# Optimizing a Trainium2 kernel written in Bass

```python
import numpy as np
import jax
import jax.numpy as jnp

def _softmax(x, axis=-1):
    return jax.nn.softmax(x, axis=axis)

def _gelu(x):
    return jax.nn.gelu(x, approximate=True)

def _silu(x):
    return jax.nn.silu(x)

def _sigmoid(x):
    return jax.nn.sigmoid(x)

def _layernorm(x, axis=-1, eps=1e-05):
    m = jnp.mean(x, axis=axis, keepdims=True)
    v = jnp.var(x, axis=axis, keepdims=True)
    return (x - m) / jnp.sqrt(v + eps)

def _scatter_add(tgt, idx, src, axis=0):
    return tgt.at[idx].add(src)

def _segment_sum(src, seg, n):
    return jax.ops.segment_sum(src, seg, n)
kernel_name = 'mk_seq_preln_d2_jaxref_r8_906340'

def setup_inputs(seed: int=0):
    np.random.seed(seed)
    _w = jnp.asarray

    def _L0_attn_setup():
        import jax, jax.numpy as jnp
        import numpy as np
        D_MODEL = 128
        NHEAD = 16
        HEAD_DIM = D_MODEL // NHEAD
        B, L = (4, 512)
        LN_EPS = 1e-05

        def _retention(v, lam):

            def step(state, v_t):
                state = lam[None, :, None] * state + v_t
                return (state, state)
            v_l_first = jnp.swapaxes(v, 0, 1)
            init = jnp.zeros(v_l_first.shape[1:], dtype=v.dtype)
            _, states = jax.lax.scan(step, init, v_l_first)
            return jnp.swapaxes(states, 0, 1)
        key = jax.random.key(seed)
        ks = jax.random.split(key, 8)
        x = jax.random.normal(ks[0], (B, L, D_MODEL), dtype=jnp.float32)
        sin = jnp.zeros((L, HEAD_DIM), dtype=jnp.float32)
        cos = jnp.zeros((L, HEAD_DIM), dtype=jnp.float32)
        decay = jax.random.uniform(ks[1], (NHEAD, 2, 1), dtype=jnp.float32)
        scale = 0.02
        Wq = jax.random.normal(ks[2], (D_MODEL, D_MODEL), dtype=jnp.float32) * scale
        Wv = jax.random.normal(ks[3], (D_MODEL, D_MODEL), dtype=jnp.float32) * scale
        Wo = jax.random.normal(ks[4], (D_MODEL, D_MODEL), dtype=jnp.float32) * scale
        Wg = jax.random.normal(ks[5], (D_MODEL, D_MODEL), dtype=jnp.float32) * scale
        ln_g = jnp.ones((D_MODEL,), dtype=jnp.float32)
        ln_b = jnp.zeros((D_MODEL,), dtype=jnp.float32)
        return {'x': x, 'sin': sin, 'cos': cos, 'decay': decay, 'Wq': Wq, 'Wv': Wv, 'Wo': Wo, 'Wg': Wg, 'ln_g': ln_g, 'ln_b': ln_b}
    _L0_attn_in = _L0_attn_setup()

    def _L0_ffn_setup():
        import jax, jax.numpy as jnp
        import numpy as np
        DIM = 128
        DEPTH = 6
        HEADS = 16
        DIM_HEAD = 64
        WINDOW = 32
        INNER = HEADS * DIM_HEAD
        DIM_INNER = int(DIM * 4 * 2 / 3)
        QK_SCALE = 8.0

        def shift_tokens(t):
            a, s = jnp.split(t, 2, -1)
            s = jnp.pad(s, ((0, 0), (1, 0), (0, 0)))[:, :-1]
            return jnp.concatenate([a, s], -1)

        def l2norm(t):
            return t / jnp.maximum(jnp.linalg.norm(t, axis=-1, keepdims=True), 1e-12)

        def rotate_half(x):
            x1, x2 = jnp.split(x, 2, -1)
            return jnp.concatenate([-x2, x1], -1)

        def rotary_tables(n):
            half = jnp.arange(0, DIM_HEAD, 2, dtype=jnp.float32)
            inv_freq = 1.0 / 10000.0 ** (half / DIM_HEAD)
            t = jnp.arange(n, dtype=jnp.float32)
            freqs = t[:, None] * inv_freq[None, :]
            freqs = jnp.concatenate([freqs, freqs], -1)
            base_scale = (half + 0.4 * DIM_HEAD) / (1.4 * DIM_HEAD)
            power = (t - n // 2) / (WINDOW // 2)
            scale = base_scale[None, :] ** power[:, None]
            scale = jnp.concatenate([scale, scale], -1)
            return (freqs, scale)

        def local_attention(q, k, v):
            b, h, n, d = q.shape
            w = WINDOW
            nw = n // w
            bq = q.reshape(b, h, nw, w, d)
            bk = k.reshape(b, h, nw, w, d)
            bv = v.reshape(b, h, nw, w, d)

            def look(t):
                p = jnp.pad(t, ((0, 0), (0, 0), (1, 0), (0, 0), (0, 0)))
                return jnp.concatenate([p[:, :, :nw], p[:, :, 1:]], axis=3)
            bk2, bv2 = (look(bk), look(bv))
            seq = jnp.arange(n).reshape(nw, w)
            seq_p = jnp.pad(seq, ((1, 0), (0, 0)), constant_values=-1)
            jt = jnp.concatenate([seq_p[:nw], seq_p[1:]], axis=1)
            it = seq[:, :, None]
            jb = jt[:, None, :]
            mask = (it < jb) | (it > jb + w) | (jb == -1)
            sim = jnp.einsum('bhwie,bhwje->bhwij', bq, bk2) * QK_SCALE
            sim = jnp.where(mask, -jnp.finfo(sim.dtype).max, sim)
            attn = jax.nn.softmax(sim, -1)
            out = jnp.einsum('bhwij,bhwje->bhwie', attn, bv2)
            return out.reshape(b, h, n, d)

        def attn_layer(x, Wqkv, qs, ksc, Wo):
            b, n, _ = x.shape
            qkv = x @ Wqkv
            q, k, v = jnp.split(qkv, 3, -1)
            sh = lambda t: t.reshape(b, n, HEADS, DIM_HEAD).transpose(0, 2, 1, 3)
            q, k, v = (sh(q), sh(k), sh(v))
            q = l2norm(q) * qs
            k = l2norm(k) * ksc
            freqs, scale = rotary_tables(n)
            cos, sin = (jnp.cos(freqs), jnp.sin(freqs))
            q = q * cos * scale + rotate_half(q) * sin * scale
            inv = 1.0 / scale
            k = k * cos * inv + rotate_half(k) * sin * inv
            out = local_attention(q, k, v)
            out = out.transpose(0, 2, 1, 3).reshape(b, n, INNER)
            return out @ Wo

        def ffn_layer(x, g, bln, W1, b1, W2, b2):
            mu = x.mean(-1, keepdims=True)
            var = ((x - mu) ** 2).mean(-1, keepdims=True)
            xn = (x - mu) / jnp.sqrt(var + 1e-05) * g + bln
            hg = xn @ W1 + b1
            a, gate = jnp.split(hg, 2, -1)
            return a * jax.nn.gelu(gate, approximate=False) @ W2 + b2
        key = jax.random.key(seed)
        ks = jax.random.split(key, 8)
        B, N = (2, 256)
        init = lambda k, shape: jax.random.normal(k, shape, jnp.float32) * 0.02
        return {'x': jax.random.normal(ks[0], (B, N, DIM), jnp.float32), 'Wqkv': init(ks[1], (DEPTH, DIM, 3 * INNER)), 'q_scale': jnp.ones((DEPTH, DIM_HEAD), jnp.float32), 'k_scale': jnp.ones((DEPTH, DIM_HEAD), jnp.float32), 'Wo': init(ks[2], (DEPTH, INNER, DIM)), 'ln_g': jnp.ones((DEPTH, DIM), jnp.float32), 'ln_b': jnp.zeros((DEPTH, DIM), jnp.float32), 'W1': init(ks[3], (DEPTH, DIM, 2 * DIM_INNER)), 'b1': jnp.zeros((DEPTH, 2 * DIM_INNER), jnp.float32), 'W2': init(ks[4], (DEPTH, DIM_INNER, DIM)), 'b2': jnp.zeros((DEPTH, DIM), jnp.float32)}
    _L0_ffn_in = _L0_ffn_setup()

    def _L1_attn_setup():
        import math
        import jax, jax.numpy as jnp
        import numpy as np
        N_HEADS = 16
        CHUNK = 64

        def _chunked_causal_attention(q, k, v, chunk=CHUNK):
            B, H, S, D = q.shape
            scale = 1.0 / math.sqrt(D)
            nc = S // chunk
            qc = jnp.moveaxis(q.reshape(B, H, nc, chunk, D), 2, 0)
            kpos = jnp.arange(S)

            def body(_, inp):
                qi, ci = inp
                scores = jnp.einsum('bhcd,bhsd->bhcs', qi, k) * scale
                qpos = ci * chunk + jnp.arange(chunk)
                mask = kpos[None, :] <= qpos[:, None]
                scores = jnp.where(mask, scores, jnp.finfo(scores.dtype).min)
                p = jax.nn.softmax(scores, axis=-1)
                return (None, jnp.einsum('bhcs,bhsd->bhcd', p, v))
            _, outs = jax.lax.scan(body, None, (qc, jnp.arange(nc)))
            return jnp.moveaxis(outs, 0, 2).reshape(B, H, S, D)
        key = jax.random.key(seed)
        kx, kq, kk, kv, ko = jax.random.split(key, 5)
        d = 128
        x = jax.random.normal(kx, (1, 512, d), dtype=jnp.float32)
        Wq = jax.random.normal(kq, (d, d), dtype=jnp.float32) * 0.02
        Wk = jax.random.normal(kk, (d, d), dtype=jnp.float32) * 0.02
        Wv = jax.random.normal(kv, (d, d), dtype=jnp.float32) * 0.02
        Wo = jax.random.normal(ko, (d, d), dtype=jnp.float32) * 0.02
        return {'x': x, 'Wq': Wq, 'Wk': Wk, 'Wv': Wv, 'Wo': Wo}
    _L1_attn_in = _L1_attn_setup()

    def _L1_ffn_setup():
        import jax, jax.numpy as jnp
        import numpy as np
        D, H, O, E, TOPK = (128, 512, 128, 8, 2)
        B, S = (4, 128)
        key = jax.random.key(seed)
        ks = jax.random.split(key, 12)
        std = 0.02
        return {'hidden_states': jax.random.normal(ks[0], (B, S, D), dtype=jnp.float32), 'norm_weight': jnp.ones((D,), dtype=jnp.float32), 'router_w': jax.random.normal(ks[1], (E, D), dtype=jnp.float32) * std, 'sw1': jax.random.normal(ks[2], (D, H), dtype=jnp.float32) * (1.0 / np.sqrt(D)), 'sb1': jnp.zeros((H,), dtype=jnp.float32), 'sw2': jax.random.normal(ks[3], (H, O), dtype=jnp.float32) * (1.0 / np.sqrt(H)), 'sb2': jnp.zeros((O,), dtype=jnp.float32), 'ew1': jax.random.normal(ks[4], (E, D, H), dtype=jnp.float32) * (1.0 / np.sqrt(D)), 'eb1': jnp.zeros((E, H), dtype=jnp.float32), 'ew2': jax.random.normal(ks[5], (E, H, O), dtype=jnp.float32) * (1.0 / np.sqrt(H)), 'eb2': jnp.zeros((E, O), dtype=jnp.float32)}
    _L1_ffn_in = _L1_ffn_setup()
    _d = {'L0_attn_x': _L0_attn_in['x'], 'L0_attn_sin': _L0_attn_in['sin'], 'L0_attn_cos': _L0_attn_in['cos'], 'L0_attn_decay': _L0_attn_in['decay'], 'L0_attn_Wq': _L0_attn_in['Wq'], 'L0_attn_Wv': _L0_attn_in['Wv'], 'L0_attn_Wo': _L0_attn_in['Wo'], 'L0_attn_Wg': _L0_attn_in['Wg'], 'L0_attn_ln_g': _L0_attn_in['ln_g'], 'L0_attn_ln_b': _L0_attn_in['ln_b'], 'L0_ffn_Wqkv': _L0_ffn_in['Wqkv'], 'L0_ffn_q_scale': _L0_ffn_in['q_scale'], 'L0_ffn_k_scale': _L0_ffn_in['k_scale'], 'L0_ffn_Wo': _L0_ffn_in['Wo'], 'L0_ffn_ln_g': _L0_ffn_in['ln_g'], 'L0_ffn_ln_b': _L0_ffn_in['ln_b'], 'L0_ffn_W1': _L0_ffn_in['W1'], 'L0_ffn_b1': _L0_ffn_in['b1'], 'L0_ffn_W2': _L0_ffn_in['W2'], 'L0_ffn_b2': _L0_ffn_in['b2'], 'L1_attn_Wq': _L1_attn_in['Wq'], 'L1_attn_Wk': _L1_attn_in['Wk'], 'L1_attn_Wv': _L1_attn_in['Wv'], 'L1_attn_Wo': _L1_attn_in['Wo'], 'L1_ffn_norm_weight': _L1_ffn_in['norm_weight'], 'L1_ffn_router_w': _L1_ffn_in['router_w'], 'L1_ffn_sw1': _L1_ffn_in['sw1'], 'L1_ffn_sb1': _L1_ffn_in['sb1'], 'L1_ffn_sw2': _L1_ffn_in['sw2'], 'L1_ffn_sb2': _L1_ffn_in['sb2'], 'L1_ffn_ew1': _L1_ffn_in['ew1'], 'L1_ffn_eb1': _L1_ffn_in['eb1'], 'L1_ffn_ew2': _L1_ffn_in['ew2'], 'L1_ffn_eb2': _L1_ffn_in['eb2']}
    _x0 = _d['L0_attn_x']
    _d['L0_attn_x'] = jax.random.normal(jax.random.fold_in(jax.random.key(seed), 1), (2, 2048, 128), dtype=_x0.dtype)
    del _x0
    return _d

def reference(L0_attn_x, L0_attn_sin, L0_attn_cos, L0_attn_decay, L0_attn_Wq, L0_attn_Wv, L0_attn_Wo, L0_attn_Wg, L0_attn_ln_g, L0_attn_ln_b, L0_ffn_Wqkv, L0_ffn_q_scale, L0_ffn_k_scale, L0_ffn_Wo, L0_ffn_ln_g, L0_ffn_ln_b, L0_ffn_W1, L0_ffn_b1, L0_ffn_W2, L0_ffn_b2, L1_attn_Wq, L1_attn_Wk, L1_attn_Wv, L1_attn_Wo, L1_ffn_norm_weight, L1_ffn_router_w, L1_ffn_sw1, L1_ffn_sb1, L1_ffn_sw2, L1_ffn_sb2, L1_ffn_ew1, L1_ffn_eb1, L1_ffn_ew2, L1_ffn_eb2):

    def _L0_attn_ref(x, sin, cos, decay, Wq, Wv, Wo, Wg, ln_g, ln_b):
        import jax, jax.numpy as jnp
        import numpy as np
        D_MODEL = 128
        NHEAD = 16
        HEAD_DIM = D_MODEL // NHEAD
        B, L = (4, 512)
        LN_EPS = 1e-05

        def _retention(v, lam):

            def step(state, v_t):
                state = lam[None, :, None] * state + v_t
                return (state, state)
            v_l_first = jnp.swapaxes(v, 0, 1)
            init = jnp.zeros(v_l_first.shape[1:], dtype=v.dtype)
            _, states = jax.lax.scan(step, init, v_l_first)
            return jnp.swapaxes(states, 0, 1)
        del sin, cos
        Bx, Lx, D = x.shape
        H = decay.shape[0]
        Dh = D // H
        q = (x @ Wq.T).reshape(Bx, Lx, H, Dh)
        v = (x @ Wv.T).reshape(Bx, Lx, H, Dh)
        lam = decay[:, 1, 0]
        state = _retention(v, lam)
        y = (q * state).reshape(Bx, Lx, D)
        mu = jnp.mean(y, axis=-1, keepdims=True)
        var = jnp.mean(jnp.square(y - mu), axis=-1, keepdims=True)
        y = (y - mu) * jax.lax.rsqrt(var + LN_EPS) * ln_g + ln_b
        gate = jax.nn.silu(x @ Wg.T)
        y = y * gate
        return y @ Wo.T

    def _L0_ffn_ref(x, Wqkv, q_scale, k_scale, Wo, ln_g, ln_b, W1, b1, W2, b2):
        import jax, jax.numpy as jnp
        import numpy as np
        DIM = 128
        DEPTH = 6
        HEADS = 16
        DIM_HEAD = 64
        WINDOW = 32
        INNER = HEADS * DIM_HEAD
        DIM_INNER = int(DIM * 4 * 2 / 3)
        QK_SCALE = 8.0

        def shift_tokens(t):
            a, s = jnp.split(t, 2, -1)
            s = jnp.pad(s, ((0, 0), (1, 0), (0, 0)))[:, :-1]
            return jnp.concatenate([a, s], -1)

        def l2norm(t):
            return t / jnp.maximum(jnp.linalg.norm(t, axis=-1, keepdims=True), 1e-12)

        def rotate_half(x):
            x1, x2 = jnp.split(x, 2, -1)
            return jnp.concatenate([-x2, x1], -1)

        def rotary_tables(n):
            half = jnp.arange(0, DIM_HEAD, 2, dtype=jnp.float32)
            inv_freq = 1.0 / 10000.0 ** (half / DIM_HEAD)
            t = jnp.arange(n, dtype=jnp.float32)
            freqs = t[:, None] * inv_freq[None, :]
            freqs = jnp.concatenate([freqs, freqs], -1)
            base_scale = (half + 0.4 * DIM_HEAD) / (1.4 * DIM_HEAD)
            power = (t - n // 2) / (WINDOW // 2)
            scale = base_scale[None, :] ** power[:, None]
            scale = jnp.concatenate([scale, scale], -1)
            return (freqs, scale)

        def local_attention(q, k, v):
            b, h, n, d = q.shape
            w = WINDOW
            nw = n // w
            bq = q.reshape(b, h, nw, w, d)
            bk = k.reshape(b, h, nw, w, d)
            bv = v.reshape(b, h, nw, w, d)

            def look(t):
                p = jnp.pad(t, ((0, 0), (0, 0), (1, 0), (0, 0), (0, 0)))
                return jnp.concatenate([p[:, :, :nw], p[:, :, 1:]], axis=3)
            bk2, bv2 = (look(bk), look(bv))
            seq = jnp.arange(n).reshape(nw, w)
            seq_p = jnp.pad(seq, ((1, 0), (0, 0)), constant_values=-1)
            jt = jnp.concatenate([seq_p[:nw], seq_p[1:]], axis=1)
            it = seq[:, :, None]
            jb = jt[:, None, :]
            mask = (it < jb) | (it > jb + w) | (jb == -1)
            sim = jnp.einsum('bhwie,bhwje->bhwij', bq, bk2) * QK_SCALE
            sim = jnp.where(mask, -jnp.finfo(sim.dtype).max, sim)
            attn = jax.nn.softmax(sim, -1)
            out = jnp.einsum('bhwij,bhwje->bhwie', attn, bv2)
            return out.reshape(b, h, n, d)

        def attn_layer(x, Wqkv, qs, ksc, Wo):
            b, n, _ = x.shape
            qkv = x @ Wqkv
            q, k, v = jnp.split(qkv, 3, -1)
            sh = lambda t: t.reshape(b, n, HEADS, DIM_HEAD).transpose(0, 2, 1, 3)
            q, k, v = (sh(q), sh(k), sh(v))
            q = l2norm(q) * qs
            k = l2norm(k) * ksc
            freqs, scale = rotary_tables(n)
            cos, sin = (jnp.cos(freqs), jnp.sin(freqs))
            q = q * cos * scale + rotate_half(q) * sin * scale
            inv = 1.0 / scale
            k = k * cos * inv + rotate_half(k) * sin * inv
            out = local_attention(q, k, v)
            out = out.transpose(0, 2, 1, 3).reshape(b, n, INNER)
            return out @ Wo

        def ffn_layer(x, g, bln, W1, b1, W2, b2):
            mu = x.mean(-1, keepdims=True)
            var = ((x - mu) ** 2).mean(-1, keepdims=True)
            xn = (x - mu) / jnp.sqrt(var + 1e-05) * g + bln
            hg = xn @ W1 + b1
            a, gate = jnp.split(hg, 2, -1)
            return a * jax.nn.gelu(gate, approximate=False) @ W2 + b2
        for i in range(DEPTH):
            x = attn_layer(shift_tokens(x), Wqkv[i], q_scale[i], k_scale[i], Wo[i]) + x
            x = ffn_layer(shift_tokens(x), ln_g[i], ln_b[i], W1[i], b1[i], W2[i], b2[i]) + x
        return x

    def _L1_attn_ref(x, Wq, Wk, Wv, Wo):
        import math
        import jax, jax.numpy as jnp
        import numpy as np
        N_HEADS = 16
        CHUNK = 64

        def _chunked_causal_attention(q, k, v, chunk=CHUNK):
            B, H, S, D = q.shape
            scale = 1.0 / math.sqrt(D)
            nc = S // chunk
            qc = jnp.moveaxis(q.reshape(B, H, nc, chunk, D), 2, 0)
            kpos = jnp.arange(S)

            def body(_, inp):
                qi, ci = inp
                scores = jnp.einsum('bhcd,bhsd->bhcs', qi, k) * scale
                qpos = ci * chunk + jnp.arange(chunk)
                mask = kpos[None, :] <= qpos[:, None]
                scores = jnp.where(mask, scores, jnp.finfo(scores.dtype).min)
                p = jax.nn.softmax(scores, axis=-1)
                return (None, jnp.einsum('bhcs,bhsd->bhcd', p, v))
            _, outs = jax.lax.scan(body, None, (qc, jnp.arange(nc)))
            return jnp.moveaxis(outs, 0, 2).reshape(B, H, S, D)
        B, S, D = x.shape
        H = N_HEADS
        hd = D // H
        q = (x @ Wq.T).reshape(B, S, H, hd).transpose(0, 2, 1, 3)
        k = (x @ Wk.T).reshape(B, S, H, hd).transpose(0, 2, 1, 3)
        v = (x @ Wv.T).reshape(B, S, H, hd).transpose(0, 2, 1, 3)
        out = _chunked_causal_attention(q, k, v)
        out = out.transpose(0, 2, 1, 3).reshape(B, S, D)
        return out @ Wo.T

    def _L1_ffn_ref(hidden_states, norm_weight, router_w, sw1, sb1, sw2, sb2, ew1, eb1, ew2, eb2):
        import jax, jax.numpy as jnp
        import numpy as np
        D, H, O, E, TOPK = (128, 512, 128, 8, 2)
        B, S = (4, 128)
        b, s, d = hidden_states.shape
        var = jnp.mean(jnp.square(hidden_states), axis=-1, keepdims=True)
        normed = hidden_states * jax.lax.rsqrt(var + 1e-08) * norm_weight
        shared = jnp.maximum(normed @ sw1 + sb1, 0.0) @ sw2 + sb2
        flat = normed.reshape(-1, d)
        T = flat.shape[0]
        probs = jax.nn.sigmoid(flat @ router_w.T)
        scores, idx = jax.lax.top_k(probs, TOPK)
        w = scores / (jnp.sum(scores, axis=-1, keepdims=True) + 1e-06)
        comb = jnp.zeros((T, E), dtype=flat.dtype)
        comb = comb.at[jnp.arange(T)[:, None], idx].add(w)
        h = jnp.maximum(jnp.einsum('td,edh->teh', flat, ew1) + eb1[None, :, :], 0.0)
        eo = jnp.einsum('teh,eho->teo', h, ew2) + eb2[None, :, :]
        routed = jnp.einsum('teo,te->to', eo, comb)
        return shared + routed.reshape(b, s, -1)
    x = L0_attn_x
    x = x + _L0_attn_ref(_layernorm(x, axis=-1), L0_attn_sin, L0_attn_cos, L0_attn_decay, L0_attn_Wq, L0_attn_Wv, L0_attn_Wo, L0_attn_Wg, L0_attn_ln_g, L0_attn_ln_b)
    x = x + _L0_ffn_ref(_layernorm(x, axis=-1), L0_ffn_Wqkv, L0_ffn_q_scale, L0_ffn_k_scale, L0_ffn_Wo, L0_ffn_ln_g, L0_ffn_ln_b, L0_ffn_W1, L0_ffn_b1, L0_ffn_W2, L0_ffn_b2)
    x = x + _L1_attn_ref(_layernorm(x, axis=-1), L1_attn_Wq, L1_attn_Wk, L1_attn_Wv, L1_attn_Wo)
    x = x + _L1_ffn_ref(_layernorm(x, axis=-1), L1_ffn_norm_weight, L1_ffn_router_w, L1_ffn_sw1, L1_ffn_sb1, L1_ffn_sw2, L1_ffn_sb2, L1_ffn_ew1, L1_ffn_eb1, L1_ffn_ew2, L1_ffn_eb2)
    return x

_drawn_inputs = setup_inputs


def setup_inputs(seed=0):
    import zlib

    import numpy as np

    out = dict(_drawn_inputs(seed))
    spreads = {'L0_attn_sin': (0.0, 0.1),
     'L0_attn_cos': (0.0, 0.1),
     'L0_attn_ln_g': (1.0, 0.6),
     'L0_attn_ln_b': (0.0, 0.706),
     'L0_ffn_q_scale': (1.0, 0.6),
     'L0_ffn_k_scale': (1.0, 0.6),
     'L0_ffn_ln_g': (1.0, 0.6),
     'L0_ffn_ln_b': (0.0, 0.612),
     'L0_ffn_b1': (0.0, 0.323),
     'L0_ffn_b2': (0.0, 0.1),
     'L1_ffn_norm_weight': (1.0, 0.2),
     'L1_ffn_sb1': (0.0, 0.1),
     'L1_ffn_sb2': (0.0, 0.1),
     'L1_ffn_eb1': (0.0, 0.372),
     'L1_ffn_eb2': (0.0, 0.1)}
    factors = {'L1_attn_Wq': 8.0, 'L1_attn_Wk': 8.0, 'L1_attn_Wv': 4.325, 'L1_attn_Wo': 4.814}
    for name, (base, spread) in spreads.items():
        noise = np.random.default_rng([zlib.crc32(name.encode()), seed]).standard_normal(out[name].shape)
        drawn = base * np.exp(spread * noise) if base else spread * noise
        out[name] = jnp.asarray(drawn.astype(out[name].dtype))
    for name, factor in factors.items():
        out[name] = (out[name] * factor).astype(out[name].dtype)
    return out
```

```python
import concourse.bass as bass
from concourse import mybir
from contextlib import ExitStack


def build_program(nc, t, out, scr):
    fp32 = mybir.dt.float32
    bf16 = mybir.dt.bfloat16
    ALU = mybir.AluOpType
    ACT = mybir.ActivationFunctionType
    AX = mybir.AxisListType

    P = 128
    D = 128
    BATCH, SEQ = 2, 2048
    CH = 512
    NC = BATCH * SEQ // CH
    CB = SEQ // CH
    NBLK = CH // P
    WIN = 32
    NWIN = CH // WIN
    DH = 64
    DEPTH = 6
    PAIRS = 8
    UNITS = NC
    PADC = WIN + 1
    EPS = 1e-5
    FF = 341
    FT = [(0, 128), (128, 128), (256, 85)]

    ctx = ExitStack()
    with ctx:
        def sb(name, shape, dt=fp32):
            return ctx.enter_context(nc.sbuf_tensor(name, shape, dt))

        def sem(name):
            return ctx.enter_context(nc.semaphore(name))

        X = sb("X", [P, NC * CH])
        XL = sb("XL", [P, BATCH, PADC + SEQ])
        XN = sb("XN", [P, BATCH, PADC + SEQ])
        TOK = sb("TOK", [P, NC * NBLK, P])
        XC = sb("XC", [P, NC * CH])
        RA = sb("RA", [P, NC * CH])
        RB = sb("RB", [P, NC * CH])
        SQ = sb("SQ", [P, 2, CH])
        NCON = 128 + 128 + 32 + 1 + 128
        con = sb("con", [P, NCON])
        ident = con[:, 0:128]
        mean_w = con[:, 128:256]
        headsel = con[:, 256:288]
        carry_f = con[:, 288:289]
        mask_f = con[:, 289:417]
        ident_b = sb("ident_b", [P, P], bf16)
        mask_b = sb("mask_b", [P, 2, CH // 2], bf16)
        var_s = sb("var_s", [P, 2, NBLK])
        rstd = sb("rstd", [P, 2, NBLK])
        mhalf = sb("mhalf", [P, 16])
        wA = sb("wA", [P, 4, D])
        vecA = sb("vecA", [P, 3])
        wqkv = sb("wqkv", [P, 3 * P])
        wo = sb("wo", [P, D])
        qks = sb("qks", [P, 4])
        xs = sb("xs", [P, 2, WIN + CH])
        tq = sb("tq", [P, 2, CH])
        tk = sb("tk", [P, 2, CH])
        ksum = sb("ksum", [P, CH])
        qT = sb("qT", [P, 2, CH])
        kT = sb("kT", [P, 2, WIN + CH])
        sqh = sb("sqh", [P, 2, CH])
        ssT = sb("ssT", [64, CH])
        ss = sb("ss", [P, 16])
        rn = sb("rn", [P, 2, 16])
        rnx = sb("rnx", [P, NBLK, P])
        mx = sb("mx", [P, 8])
        S1 = sb("S1", [P, CH])
        S2 = sb("S2", [P, CH])
        EX = sb("EX", [P, CH])
        rs = sb("rs", [P, 8])
        rr = sb("rr", [P, 8])
        PN = sb("PN", [P, CH])
        PT = sb("PT", [P, CH])
        V2 = sb("V2", [P, 2, NWIN * DH])
        oT = sb("oT", [P, CH])
        w1 = sb("w1", [P, 2 * FF])
        w2 = sb("w2", [P, 3, D])
        fvec = sb("fvec", [P, 9])
        gl = sb("gl", [P, 2, CH])
        hh = sb("hh", [P, 6, CH])

        PB = [None, None] + [ctx.enter_context(nc.psum_tensor(f"PB{i}", [P, CH], fp32)) for i in range(2, 6)]
        QS = ctx.enter_context(nc.psum_tensor("QS", [P, 2 * CH], fp32))
        PB = PB + [QS[:, 0:CH], QS[:, CH:2 * CH]]
        QS01 = ctx.enter_context(nc.psum_tensor("QS01", [P, 2 * CH], fp32))
        PB[0], PB[1] = QS01[:, 0:CH], QS01[:, CH:2 * CH]
        ST2 = [QS01[:, :].rearrange("p (h n) -> p h n", h=2), QS[:, :].rearrange("p (h n) -> p h n", h=2)]
        TABQ = RA[:, :].rearrange("p (a n) -> p a n", a=2)
        TABK = RB[:, :].rearrange("p (a n) -> p a n", a=2)
        XS = TOK[:, :, :].rearrange("p a b -> p (a b)")

        def chunk(buf, c):
            return buf[:, c * CH:(c + 1) * CH]

        def inner(buf, c):
            b, j = divmod(c, CB)
            return buf[:, b, PADC + j * CH:PADC + (j + 1) * CH]

        HD = 8
        GH = 4
        NG = 8
        NT = SEQ // P
        PARTS = 3
        KR = PARTS * PARTS * HD
        wC = sb("wC", [P, 4, D])
        tri_q = sb("tri_q", [P, P], bf16)
        tri_k = sb("tri_k", [P, P], bf16)
        mxp = sb("mxp", [P, GH, NT, CB])
        mxa = sb("mxa", [P, GH * NT])
        nhi = sb("nhi", [P, GH * NT], bf16)
        nmid = sb("nmid", [P, GH * NT], bf16)
        nparts = sb("nparts", [P, 4, GH * NT])
        nrest = sb("nrest", [P, 2, GH * NT])
        nT = sb("nT", [P, 2, P], bf16)
        o_inv = sb("o_inv", [P, 16])
        QST = [r[:, :].bitcast(bf16) for r in (RA, RB)]
        KST = [TOK[:, :, :].rearrange("p a b -> p (a b)").bitcast(bf16), XC[:, :].bitcast(bf16)]
        VALL = XL[:, :, :].rearrange("p a n -> p (a n)")[:, 0:NC * CH].rearrange("p (n f) -> p n f", f=D)
        OTOK = XN[:, :, :].rearrange("p a n -> p (a n)")[:, 0:NC * CH].rearrange("p (n f) -> p n f", f=D)
        SPL = hh[:, :, :].rearrange("p a n -> p (a n)").bitcast(bf16).rearrange("p (a q s n) -> p a q s n", a=2, q=2, s=3)
        REST = V2[:, :, :].rearrange("p a (q n) -> p a q n", q=2)
        PTE = [hh[:, 0:4, :], V2[:, :, :].rearrange("p a (q n) -> p (a q) n", q=2)]
        VG = [r[:, :, :].rearrange("p a n -> p (a n)")[:, 0:GH * NT * 9].rearrange("p (h b f) -> p h b f", h=GH, f=9)
              for r in (tq, tk)]
        oTs = oT[:, :]
        NE = 8
        HF = 4
        mvec = sb("mvec", [P, 37])
        bias2 = sb("bias2", [9, D])
        routw = sb("routw", [P, NE])
        tri_e = sb("tri_e", [P, NE, NE])
        PR = sb("PR", [P, NC * NBLK, NE])
        CM = sb("CM", [P, NC * NBLK, NE + 1])
        RK = [sb(f"RK{i}", [P, NC * NBLK, NE]) for i in range(2)]
        wsum = sb("wsum", [P, NC * NBLK])
        cmc = sb("cmc", [P, NBLK, NE + 1])
        cmT = ssT[0:9, :]
        EW1 = RA[:, :].rearrange("p (e n) -> p e n", e=NE)
        EW2 = RB[:, :].rearrange("p (e k n) -> p e k n", e=NE, k=HF)
        SW1 = S1[:, :]
        SW2 = S2[:, :].rearrange("p (k n) -> p k n", k=HF)
        HB = [XC[:, 0:2048].rearrange("p (k n) -> p k n", k=HF), XC[:, 2048:4096].rearrange("p (k n) -> p k n", k=HF),
              V2[:, :, :].rearrange("p a (q n) -> p (a q) n", q=2)]
        CMPA = hh[:, 0:4, :].rearrange("p a n -> p (a n)").rearrange("p (t e j) -> p t e j", e=NE, j=NE)
        CMPB = V2[:, :, :].rearrange("p a n -> p (a n)").rearrange("p (t e j) -> p t e j", e=NE, j=NE)
        XTOK = OTOK
        ACC = EX[:, :].rearrange("p (b n) -> p b n", b=NBLK)
        OUTB = PN[:, :].rearrange("p (b n) -> p b n", b=NBLK)

        s = {n: sem(n) for n in (
            "const_in", "const_ready", "x_in", "wA_in", "tables_in", "x_blocks", "x_turned",
            "mean_ready", "centered", "squared", "var_ready", "var_copied", "rstd_ready", "spread_ready",
            "normed", "scaled", "projA_ready", "scanned", "gated", "silu_ready", "gatedmul", "outA_ready", "x1_ready",
            "inner_copied", "pads_zero",
            "pair_in", "wo_in", "qks_in", "ffw_in",
            "xs_ready", "projq", "projk", "rotq", "rotk", "qsum", "ksumd", "sqq", "sqd", "swapq", "swapk", "ssrow", "sscopy", "ssq", "ssc", "rnorm", "rnwide",
            "spreadk", "kready", "scores", "maxed", "shifted", "scaledS", "exped", "summed", "recip", "pnorm",
            "ptrans", "ptcopy", "vproj0", "vproj1", "vcopy0", "vcopy1", "pv", "ocopy", "yproj", "acc",
            "shiftF", "affine", "up", "gelu", "hmul", "down", "layer_out",
            "w1att_in", "x2_ready", "c_proj", "c_hi", "c_rest", "c_mid", "c_low", "c_vcopy", "split_out0", "split_out1",
            "ones_ready", "sum_ones", "stacks_in0", "stacks_in1", "tri_ready", "vgroup", "score1", "max1", "max_all", "neg_hi", "neg_rest",
            "neg_mid", "neg_low", "neg_turned", "neg_copied", "neg_rows0", "neg_rows1",
            "score2", "exp2", "pv2", "o_zero", "o_copied", "o_turned", "o_inv", "o_stored",
            "oF_turned", "oF_copied", "out2", "x3_ready",
            "moew_in", "rms_scaled", "xtok_turned", "xtok_copied", "logits", "probs", "rank_gt", "rank_eq", "rank_tri",
            "rank_sum1", "rank_sum2", "rank", "chosen", "wsum", "winv", "comb",
            "comb_cur", "comb_turned", "comb_copied", "up2", "relu_a", "relu_v", "down2", "acc2", "stored")}

        CREDIT = 3

        def done(u):
            return u + 1 + CREDIT

        ITEM = [(c, kt) for c in range(CB) for kt in range(4 * c + 4)]
        ITEMS = len(ITEM)
        FIRST = [(h, qt, kc) for h in range(GH) for qt in range(NT) for kc in range(qt // 4 + 1)]
        NF = len(FIRST) // ITEMS
        assert NF * ITEMS == len(FIRST)

        def first_pass_keys(qt, kc):
            return min(CH, (qt + 1) * P - kc * CH)

        block = ctx.enter_context(nc.Block())

        def ends_chunk(n):
            return ITEM[n][1] == 4 * ITEM[n][0] + 3

        def norm_tensor(pe, k, src, src_sem, src_at, center=True):
            for c in range(NC if center else 0):
                pe.wait_ge(s[src_sem], src_at(c))
                if c >= 2:
                    pe.wait_ge(s["centered"], k * NC + c - 1)
                pe.matmul(PB[c % 2][:, :], mean_w, src(c), start=True, stop=True).then_inc(s["mean_ready"], 1)
            for c in range(NC):
                pe.wait_ge(s["squared"], k * NC + c + 1)
                if c >= 2:
                    pe.wait_ge(s["var_copied"], k * NC + c - 1)
                for j in range(NBLK):
                    m = pe.matmul(PB[2 + c % 2][:, j:j + 1], SQ[:, c % 2, j * P:(j + 1) * P], mean_w[:, 0:1],
                                  start=True, stop=True)
                m.then_inc(s["var_ready"], 1)
                if c >= 1:
                    spread(pe, k, c - 1)
            spread(pe, k, NC - 1)

        def spread(pe, k, c):
            pe.wait_ge(s["rstd_ready"], k * NC + c + 1)
            if c >= 2:
                pe.wait_ge(s["normed"], k * NC + c - 1)
            elif k < K_RMS:
                pe.wait_ge(s["centered"], k * NC + NC - 1 + c)
            for j in range(NBLK):
                m = pe.transpose(PB[c % 2][:, j * P:(j + 1) * P], rstd[:, c % 2, j:j + 1].to_broadcast([P, P]), ident)
            m.then_inc(s["spread_ready"], 1)

        def norm_vector(dve, k, src, dst, after=None, center=True, eps=EPS):
            for c in range(NC if center else 0):
                dve.wait_ge(s["mean_ready"], k * NC + c + 1)
                dve.tensor_tensor(dst(c), src(c), PB[c % 2][:, :], ALU.subtract).then_inc(s["centered"], 1)
            for c in range(NC):
                dve.wait_ge(s["var_ready"], k * NC + c + 1)
                if c >= 2:
                    dve.wait_ge(s["rstd_ready"], k * NC + c - 1)
                dve.tensor_scalar(var_s[:, c % 2, :], PB[2 + c % 2][:, 0:NBLK], eps, None, ALU.add).then_inc(s["var_copied"], 1)
                if c >= 1:
                    norm_apply(dve, k, c - 1, src if not center else dst, dst, after)
            norm_apply(dve, k, NC - 1, src if not center else dst, dst, after)

        def norm_apply(dve, k, c, cen, dst, after):
            dve.wait_ge(s["spread_ready"], k * NC + c + 1)
            dve.tensor_tensor(dst(c), cen(c), PB[c % 2][:, :], ALU.mult).then_inc(s["normed"], 1)
            if after:
                after(c)

        def norm_scalar(act, k, dst, ready="centered"):
            for c in range(NC):
                act.wait_ge(s[ready], (k if ready == "centered" else k - 1) * NC + c + 1)
                if c >= 2:
                    act.wait_ge(s["var_ready"], k * NC + c - 1)
                elif ready == "normed":
                    act.wait_ge(s["var_ready"], k * NC)
                act.activation(SQ[:, c % 2, :], dst(c), ACT.Square).then_inc(s["squared"], 1)

        def norm_pool(pool, k):
            for c in range(NC):
                pool.wait_ge(s["var_copied"], k * NC + c + 1)
                if c >= 2:
                    pool.wait_ge(s["spread_ready"], k * NC + c - 1)
                pool.tensor_tensor(rstd[:, c % 2, :], var_s[:, c % 2, :], mhalf[:, 0:NBLK], ALU.pow).then_inc(s["rstd_ready"], 1)

        def run_units(eng, l, step, lag):
            base = l * (PAIRS * UNITS)
            for i in range(UNITS):
                if lag == 1:
                    step(base + i, i, i == 0, False)
                else:
                    step(base + i, i, i, False)
            with eng.Fori(1, PAIRS) as pr:
                for i in range(UNITS):
                    u = base + pr * UNITS + i
                    if lag == 1:
                        step(u, i, False, False)
                    else:
                        step(u, i, 2, False)
            for i in range(lag):
                u = base + PAIRS * UNITS + i
                if lag == 1:
                    step(u, i, False, True)
                else:
                    step(u, i, 2, 1 + i)

        K_LAYER = 3
        K_ATT = K_LAYER + DEPTH
        K_MOE = K_ATT + 1
        K_RMS = K_ATT + 2

        def layer_result(dve, l, c):
            dve.wait_ge(s["down"], l * NC + c + 1)
            dve.scalar_tensor_tensor(inner(XL, c), PB[4 + c % 2][:, :], fvec[:, 8:9], inner(XN, c), ALU.add, ALU.add)\
               .then_inc(s["layer_out"], 1)

        def down(pe, l, c):
                pe.wait_ge(s["hmul"], l * (3 * NC) + c * 3 + 3 + 2)
                if c >= 2:
                    pe.wait_ge(s["layer_out"], l * NC + c - 1 + 1)
                for f, (f0, fn) in enumerate(FT):
                    m = pe.matmul(PB[4 + c % 2][:, :], w2[0:fn, f, :], hh[0:fn, (c % 2) * 3 + f, :],
                                  start=(f == 0), stop=(f == 2))
                m.then_inc(s["down"], 1)

        @block.sync
        def _(sp):
            sp.dma_start(con[:, :], t["con"]).then_inc(s["const_in"], 16)
            sp.dma_start(TOK[:, :, :], t["x"].rearrange("(n p) d -> p n d", p=P)).then_inc(s["x_in"], 16)
            sp.dma_start(wA[:, :, :], t["wA"]).then_inc(s["wA_in"], 16)
            sp.dma_start(vecA[:, :], t["vecA"]).then_inc(s["wA_in"], 16)
            sp.wait_ge(s["gatedmul"], NC)
            sp.dma_start(TABQ[:, :, :], t["tabs"][0:2].rearrange("a p n -> p a n")).then_inc(s["tables_in"], 16)
            sp.dma_start(TABK[:, :, :], t["tabs"][2:4].rearrange("a p n -> p a n")).then_inc(s["tables_in"], 16)
            with sp.Fori(0, DEPTH) as l:
                sp.wait_ge(s["layer_out"], l * NC + 1)
                sp.dma_start(w1[:, :], t["W1"][bass.ds(l, 1)].rearrange("a p n -> (a p) n")).then_inc(s["ffw_in"], 16)
                sp.dma_start(w2[:, :, :], t["W2"][bass.ds(l, 1)].rearrange("a p k n -> (a p) k n")).then_inc(s["ffw_in"], 16)
                sp.dma_start(fvec[:, :], t["fvec"][bass.ds(l, 1)].rearrange("a p n -> (a p) n")).then_inc(s["ffw_in"], 16)
                sp.dma_start(qks[:, :], t["qks"][bass.ds(l, 1)].rearrange("a p n -> (a p) n")).then_inc(s["qks_in"], 16)
                with sp.Fori(0, PAIRS) as pr:
                    u0 = l * (PAIRS * UNITS) + pr * UNITS
                    sp.wait_ge(s["vproj1"], done(u0 - 1))
                    sp.wait_ge(s["projk"], done(u0 - 1))
                    row = l * PAIRS + pr
                    sp.dma_start(wqkv[:, :], t["Wqkv"][bass.ds(row, 1)].rearrange("a p n -> (a p) n")).then_inc(s["pair_in"], 16)
                    sp.wait_ge(s["yproj"], done(u0 - 1))
                    sp.dma_start(wo[:, :], t["Wo"][bass.ds(row, 1)].rearrange("a p n -> (a p) n")).then_inc(s["wo_in"], 16)
            sp.dma_start(wC[:, :, :], t["wC"]).then_inc(s["w1att_in"], 16)
            for c in range(NC):
                b, j = divmod(c, CB)
                sp.wait_ge(s["c_low"], 2 * (c + 1))
                for qk in range(2):
                    for part in range(PARTS):
                        sp.dma_start(scr[qk, b, :, part, :, j * CH:(j + 1) * CH], SPL[:, c % 2, qk, part, :])\
                          .then_inc(s[f"split_out{c % 2}"], 16)
            for p in range(2):
                sp.wait_ge(s[f"split_out{p}"], 16 * 6 * NC // 2)
            sp.wait_ge(s["ones_ready"], 2)

            def load_stacks(p, hg):
                for rep in range(PARTS):
                    sp.dma_start(QST[p][rep * 24:(rep + 1) * 24, :].rearrange("r (h n) -> r h n", h=GH),
                                 scr[0, p, bass.ds(hg * GH, GH)].rearrange("h s d n -> (s d) h n"))\
                      .then_inc(s[f"stacks_in{p}"], 16)
                    for r in range(PARTS):
                        sp.dma_start(KST[p][(rep * 3 + r) * 8:(rep * 3 + r + 1) * 8, :].rearrange("r (h n) -> r h n", h=GH),
                                     scr[1, p, bass.ds(hg * GH, GH), rep].rearrange("h d n -> d h n"))\
                          .then_inc(s[f"stacks_in{p}"], 16)

            def max_rows(p, g):
                sp.wait_ge(s["neg_copied"], g + 1)
                for part in range(PARTS):
                    sp.dma_start(QST[p][KR + part:KR + part + 1, :].rearrange("r (x n) -> r x n", n=P),
                                 nT[64 * (part % 2):64 * (part % 2) + 64, part // 2, :]).then_inc(s[f"neg_rows{p}"], 16)

            load_stacks(0, 0)
            load_stacks(1, 0)
            max_rows(0, 0)
            with sp.Fori(1, NG // 2) as i:
                max_rows(1, 2 * i - 1)
                sp.wait_ge(s["pv2"], (2 * i - 1) * ITEMS + 2)
                load_stacks(0, i)
                max_rows(0, 2 * i)
                sp.wait_ge(s["pv2"], (2 * i) * ITEMS + 2)
                load_stacks(1, i)
            max_rows(1, NG - 1)
            sp.wait_ge(s["pv2"], NG * ITEMS + 2)
            sp.dma_start(EW1, t["ew1"].rearrange("e p n -> p e n")).then_inc(s["moew_in"], 16)
            sp.dma_start(EW2, t["ew2"]).then_inc(s["moew_in"], 16)
            sp.dma_start(SW1, t["sw1"]).then_inc(s["moew_in"], 16)
            sp.dma_start(SW2, t["sw2"]).then_inc(s["moew_in"], 16)
            sp.dma_start(mvec[:, :], t["mvec"]).then_inc(s["moew_in"], 16)
            sp.dma_start(bias2[:, :], t["bias2"]).then_inc(s["moew_in"], 16)
            sp.dma_start(routw[:, :], t["routw"]).then_inc(s["moew_in"], 16)
            out_v = out.rearrange("(c b p) d -> c p b d", p=P, b=NBLK)
            with sp.Fori(0, NC) as c:
                sp.wait_ge(s["acc2"], c * (NE + 1) + NE + 1 + 3)
                sp.dma_start(out_v[bass.ds(c, 1)].rearrange("a p b d -> (a p) b d"), OUTB).then_inc(s["stored"], 16)
            sp.wait_ge(s["stored"], 16 * NC + 1)

        @block.gpsimd
        def _(pool):
            pool.memset(XL[:, :, 0:PADC], 0.0).then_inc(s["pads_zero"], 1)
            pool.memset(XN[:, :, 0:PADC], 0.0).then_inc(s["pads_zero"], 1)
            pool.memset(mhalf[:, :], -0.5).then_inc(s["pads_zero"], 1)
            pool.wait_ge(s["pads_zero"], 3)
            for name in ("qsum", "ksumd", "rnorm", "pnorm"):
                pool.sem_inc(s[name], CREDIT)
            norm_pool(pool, 0)
            norm_pool(pool, 1)
            norm_pool(pool, 2)

            def step(u, i, first, last):
                if not last:
                    pool.wait_ge(s["rotq"], done(u))
                    pool.wait_ge(s["scores"], done(u - 2))
                    pool.tensor_tensor(qT[:, i % 2, :], tq[:, 0, :], tq[:, 1, :], ALU.add).then_inc(s["qsum"], 1)
                    pool.wait_ge(s["rotk"], done(u))
                    pool.wait_ge(s["kready"], done(u - 1))
                    pool.tensor_tensor(ksum[:, :], tk[:, 0, :], tk[:, 1, :], ALU.add).then_inc(s["ksumd"], 1)
                    pool.wait_ge(s["ssc"], done(u))
                    pool.wait_ge(s["rnwide"], done(u - 2))
                    pool.wait_ge(s["scaledS"], done(u - 2))
                    pool.tensor_tensor(rn[:, i % 2, :], ss[:, :], mhalf[:, :], ALU.pow).then_inc(s["rnorm"], 1)
                if not first:
                    pool.wait_ge(s["recip"], done(u - 1))
                    pool.wait_ge(s["ptrans"], done(u - 2))
                    for h in range(2):
                        m = pool.tensor_tensor(
                            PN[:, :].rearrange("p (b h n) -> p h b n", b=NBLK, h=2)[:, h],
                            EX[:, h * 256:(h + 1) * 256].rearrange("p (b n) -> p b n", b=NBLK),
                            rr[:, h * NBLK:(h + 1) * NBLK].unsqueeze(2).to_broadcast([P, NBLK, 64]), ALU.mult)
                    m.then_inc(s["pnorm"], 1)

            with pool.Fori(0, DEPTH) as l:
                run_units(pool, l, step, 1)
                norm_pool(pool, K_LAYER + l)
            norm_pool(pool, K_ATT)
            pool.memset(tri_q[:, :], 0.0).then_inc(s["tri_ready"], 1)
            pool.memset(tri_k[:, :], 0.0).then_inc(s["tri_ready"], 1)
            pool.wait_ge(s["tri_ready"], 2)
            pool.affine_select(out=tri_q[:, :], in_=tri_q[:, :], compare_op=ALU.is_ge, fill=-1e30, base=0,
                               pattern=[[-1, P]], channel_multiplier=1).then_inc(s["tri_ready"], 1)
            pool.affine_select(out=tri_k[:, :], in_=tri_k[:, :], compare_op=ALU.is_ge, fill=-1e30, base=0,
                               pattern=[[1, P]], channel_multiplier=-1).then_inc(s["tri_ready"], 1)
            pool.wait_ge(s["tri_ready"], 4)
            pool.wait_ge(s["c_proj"], NC)
            for p in range(2):
                pool.memset(KST[p][64:96, :], 1.0).then_inc(s["ones_ready"], 1)
            pool.wait_ge(s["ones_ready"], 2)
            for p in range(2):
                pool.memset(VG[p][:, :, :, 8:9], 1.0).then_inc(s["sum_ones"], 1)
            pool.wait_ge(s["sum_ones"], 2)
            pool.wait_ge(s["c_vcopy"], NC)

            def gather_v(p, g, hg):
                if p is None:
                    return
                if not (isinstance(g, int) and g < 2):
                    pool.wait_ge(s["pv2"], (g - 1) * ITEMS + 2)
                for h in range(GH):
                    m = pool.tensor_copy(VG[p][:, h, :, 0:8],
                                         VALL[:, p * NT:(p + 1) * NT, bass.ds(hg * 32 + h * 8, 8)])
                m.then_inc(s["vgroup"], 1)

            gather_v(0, 0, 0)
            gather_v(1, 1, 0)
            with pool.Fori(1, NG // 2) as i:
                gather_v(0, 2 * i, i)
                gather_v(1, 2 * i + 1, i)
            norm_pool(pool, K_MOE)
            norm_pool(pool, K_RMS)
            pool.memset(tri_e[:, :, :], 0.0).then_inc(s["rank_tri"], 1)
            pool.memset(CM[:, :, NE:NE + 1], 1.0).then_inc(s["rank_tri"], 1)
            pool.wait_ge(s["rank_tri"], 2)
            for e in range(1, NE):
                m = pool.memset(tri_e[:, e, 0:e], 1.0)
            m.then_inc(s["rank_tri"], 1)

        @block.scalar
        def _(act):
            for name in ("xs_ready", "sqq", "sqd", "swapq", "swapk", "sscopy", "exped", "rnwide", "vcopy0", "vcopy1", "ocopy"):
                act.sem_inc(s[name], CREDIT)
            norm_scalar(act, 0, lambda c: chunk(XC, c))
            for c in range(NC):
                act.wait_ge(s["projA_ready"], c + 1)
                act.activation(chunk(RB, c), PB[4 + c % 2][:, :], ACT.Silu).then_inc(s["silu_ready"], 1)
            norm_scalar(act, 1, lambda c: chunk(XC, c))
            norm_scalar(act, 2, lambda c: inner(XL, c))
            for c in range(NC):
                act.wait_ge(s["normed"], 2 * NC + c + 1)
                act.activation(inner(XN, c), inner(XL, c), ACT.Copy).then_inc(s["inner_copied"], 1)
            act.wait_ge(s["pads_zero"], 3)

            def swap_halves(dst, bank):
                for b0 in range(0, P, 32):
                    b1 = b0 + 32 if b0 % 64 == 0 else b0 - 32
                    m = act.activation(dst[b0:b0 + 32, 1, :], bank[b1:b1 + 32, :], ACT.Copy)
                return m

            def make_xs(u, i):
                b, j = divmod(i, CB)
                act.wait_ge(s["vproj1"], done(u - 2))
                act.wait_ge(s["projk"], done(u - 2))
                act.activation(xs[0:64, i % 2, :], XL[0:64, b, 1 + j * CH:1 + j * CH + WIN + CH], ACT.Copy)
                act.activation(xs[64:128, i % 2, :], XL[64:128, b, j * CH:j * CH + WIN + CH], ACT.Copy).then_inc(s["xs_ready"], 1)

            def step(u, i, have, last):
                if not last:
                    act.wait_ge(s["projq"], done(u))
                    act.wait_ge(s["ssq"], done(u - 1))
                    act.activation(sqh[:, 0, :], PB[0][:, :], ACT.Square).then_inc(s["sqq"], 1)
                    act.wait_ge(s["qsum"], done(u - 1))
                    swap_halves(tq, PB[0]).then_inc(s["swapq"], 1)
                    act.wait_ge(s["projk"], done(u))
                    act.activation(sqh[:, 1, :], PB[1][:, :], ACT.Square).then_inc(s["sqd"], 1)
                    act.wait_ge(s["ksumd"], done(u - 1))
                    swap_halves(tk, PB[1]).then_inc(s["swapk"], 1)
                    act.wait_ge(s["ssrow"], done(u))
                    act.wait_ge(s["ssq"], done(u - 1))
                    act.activation(ssT[:, :], PB[0][0:64, :], ACT.Copy).then_inc(s["sscopy"], 1)
                    act.wait_ge(s["vproj0"], done(u))
                    act.wait_ge(s["pv"], done(u - 2))
                    act.activation(V2[:, i % 2, 0:CH], PB[4][:, :], ACT.Copy).then_inc(s["vcopy0"], 1)
                if have >= 2 or last:
                    act.wait_ge(s["pv"], done(u - 2))
                    act.wait_ge(s["yproj"], done(u - 3))
                    act.activation(oT[:, :], PB[5][:, :], ACT.Copy).then_inc(s["ocopy"], 1)
                if not last:
                    make_xs(u + 1, (i + 1) % UNITS)
                if have >= 1 and last != 2:
                    act.wait_ge(s["scaledS"], done(u - 1))
                    act.wait_ge(s["pnorm"], done(u - 2))
                    act.activation(EX[:, :], S2[:, :], ACT.Exp, scale=float(DH) ** 0.5).then_inc(s["exped"], 1)
                if not last:
                    act.wait_ge(s["rnorm"], done(u))
                    act.wait_ge(s["spreadk"], done(u - 1))
                    act.activation(rnx[:, :, :].rearrange("p b (h n) -> p b h n", h=2),
                                   rn[:, i % 2, :].rearrange("p (b x) -> p b x", b=NBLK)[:, :, 2:4]
                                   .unsqueeze(3).to_broadcast([P, NBLK, 2, 64]), ACT.Copy).then_inc(s["rnwide"], 1)
                    act.wait_ge(s["vproj1"], done(u))
                    act.activation(V2[:, i % 2, CH:2 * CH], PB[2][:, :], ACT.Copy).then_inc(s["vcopy1"], 1)

            with act.Fori(0, DEPTH) as l:
                act.wait_ge(s["layer_out"], l * NC + 1)
                base = l * (PAIRS * UNITS)
                act.wait_ge(s["vproj1"], done(base - 2))
                act.activation(xs[0:64, 0, :], XL[0:64, 0, 1:1 + WIN + CH], ACT.Copy)
                act.activation(xs[64:128, 0, :], XL[64:128, 0, 0:WIN + CH], ACT.Copy).then_inc(s["xs_ready"], 1)
                run_units(act, l, step, 2)
                for c in range(NC):
                    b, j = divmod(c, CB)
                    act.wait_ge(s["acc"], done(base + PAIRS * UNITS - 1))
                    act.activation(chunk(XS, c)[0:64, :], XN[0:64, b, PADC + j * CH:PADC + (j + 1) * CH], ACT.Copy)
                    act.activation(chunk(XS, c)[64:128, :], XN[64:128, b, PADC - 1 + j * CH:PADC - 1 + (j + 1) * CH],
                                   ACT.Copy).then_inc(s["shiftF"], 1)
                norm_scalar(act, K_LAYER + l, lambda c: chunk(XS, c))
                act.wait_ge(s["ffw_in"], (l + 1) * 48)
                for c in range(NC):
                    act.wait_ge(s["normed"], (K_LAYER + l) * NC + c + 1)
                    act.activation(chunk(XC, c), chunk(XS, c), ACT.Identity, scale=fvec[:, 0:1], bias=fvec[:, 1:2])\
                       .then_inc(s["affine"], 1)
                for c in range(NC):
                    for f, (f0, fn) in enumerate(FT):
                        n = l * (3 * NC) + c * 3 + f
                        act.wait_ge(s["up"], n + 1)
                        act.wait_ge(s["hmul"], n + 2 - 1)
                        act.activation(gl[0:fn, (c * 3 + f) % 2, :], PB[2 * ((c * 3 + f) % 2) + 1][0:fn, :], ACT.Gelu,
                                       bias=fvec[0:fn, 5 + f:6 + f]).then_inc(s["gelu"], 1)
            norm_scalar(act, K_ATT, lambda c: chunk(XC, c))
            for c in range(NC):
                act.wait_ge(s["c_proj"], c + 1)
                if c >= 2:
                    act.wait_ge(s[f"split_out{c % 2}"], 96 * (c // 2))
                for qk in range(2):
                    act.activation(SPL[:, c % 2, qk, 0, :], PB[(c % 2) * 3 + qk][:, :], ACT.Copy).then_inc(s["c_hi"], 1)
                act.activation(VALL[:, c * NBLK:(c + 1) * NBLK, :].rearrange("p b f -> p (b f)"),
                               PB[(c % 2) * 3 + 2][:, :], ACT.Copy).then_inc(s["c_vcopy"], 1)
                for qk in range(2):
                    act.wait_ge(s["c_rest"], 2 * c + qk + 1)
                    act.activation(SPL[:, c % 2, qk, 1, :], REST[:, c % 2, qk, :], ACT.Copy).then_inc(s["c_mid"], 1)

            def exps(g):
                for n, (c, kt) in enumerate(ITEM):
                    r = max(0, kt - 4 * c)
                    for half in range(2):
                        it = g * ITEMS + n
                        act.wait_ge(s["score2"], 2 * it + half + 1)
                        if half == 0:
                            act.wait_ge(s["pv2"], it + 1)
                        act.activation(PTE[n % 2][:, 2 * half:2 * half + 2, 0:CH - r * P],
                                       ST2[half][:, :, 0:CH - r * P], ACT.Exp, scale=float(HD) ** -0.5)\
                           .then_inc(s["exp2"], 1)

            act.sem_inc(s["exp2"], 2)
            exps(0)
            with act.Fori(1, NG // 2) as i:
                exps(2 * i - 1)
                exps(2 * i)
            exps(NG - 1)
            for c in range(NC):
                act.wait_ge(s["oF_turned"], c + 1)
                act.activation(chunk(XS, c), PB[c % 2][:, :], ACT.Copy).then_inc(s["oF_copied"], 1)
            norm_scalar(act, K_MOE, lambda c: chunk(XC, c))
            norm_scalar(act, K_RMS, lambda c: chunk(XC, c), ready="normed")
            act.wait_ge(s["moew_in"], 16 * 7)
            for c in range(NC):
                act.wait_ge(s["normed"], K_RMS * NC + c + 1)
                act.activation(chunk(XS, c), chunk(XS, c), ACT.Copy, scale=mvec[:, 36:37]).then_inc(s["rms_scaled"], 1)
            act.wait_ge(s["logits"], 1)
            act.activation(PR[:, :, :].rearrange("p a e -> p (a e)"), PB[6][:, 0:NC * NBLK * NE], ACT.Sigmoid)\
               .then_inc(s["probs"], 1)
            act.sem_inc(s["relu_a"], 2)
            with act.Fori(0, NC) as c:
                for f in range(NE + 1):
                    it = c * (NE + 1) + f
                    act.wait_ge(s["down2"], it + 1)
                    for j in (0, 2):
                        act.wait_ge(s["up2"], it * HF + j + 1)
                        act.activation(HB[f % 3][:, j, :], PB[j][:, :], ACT.Relu, bias=mvec[:, f * HF + j:f * HF + j + 1])\
                           .then_inc(s["relu_a"], 1)

        @block.vector
        def _(dve):
            def add_expert(c, f):
                it = c * (NE + 1) + f
                dve.wait_ge(s["down2"], it + 1 + 3)
                dve.wait_ge(s["acc2"], it + 3)
                yb = PB[4 + f % 3][:, :].rearrange("p (b n) -> p b n", b=NBLK)
                if f == 0:
                    dve.tensor_tensor(ACC, yb, XTOK[:, bass.ds(c * NBLK, NBLK), :], ALU.add).then_inc(s["acc2"], 1)
                    return
                if f == NE:
                    dve.wait_ge(s["stored"], 16 * c + 1)
                for b in range(NBLK):
                    m = dve.scalar_tensor_tensor((OUTB if f == NE else ACC)[:, b, :], yb[:, b, :], cmc[:, b, f - 1:f],
                                                 ACC[:, b, :], ALU.mult, ALU.add)
                m.then_inc(s["acc2"], 1)

            dve.sem_inc(s["stored"], 1)
            for name in ("rotq", "rotk", "ssc", "kready", "maxed", "shifted", "scaledS", "summed", "recip", "ptcopy", "acc"):
                dve.sem_inc(s[name], CREDIT)
            dve.sem_inc(s["hmul"], 2)
            dve.sem_inc(s["layer_out"], 1)
            dve.wait_ge(s["const_in"], 16)
            dve.tensor_copy(ident_b[:, :], ident)
            for v in range(2):
                m = dve.tensor_copy(mask_b[:, v, :].rearrange("p (b n) -> p b n", b=NBLK),
                                    mask_f[:, 64:128].unsqueeze(1).to_broadcast([P, NBLK, 64]))
            m.then_inc(s["const_ready"], 1)
            dve.wait_ge(s["const_ready"], 1)
            dve.tensor_copy(mask_b[:, 0, 0:64], mask_f[:, 0:64]).then_inc(s["const_ready"], 1)
            for c in range(NC):
                dve.wait_ge(s["x_blocks"], c + 1)
                dve.tensor_copy(chunk(X, c), PB[c % 2][:, :]).then_inc(s["x_turned"], 1)
            norm_vector(dve, 0, lambda c: chunk(X, c), lambda c: chunk(XC, c))
            dve.wait_ge(s["wA_in"], 32)
            dve.wait_ge(s["x_blocks"], NC)
            for c in range(NC):
                dve.wait_ge(s["projA_ready"], c + 1)
                if c % CB:
                    dve.wait_ge(s["scanned"], c)
                dve.tensor_tensor_scan(chunk(RA, c), vecA[:, 0:1].to_broadcast([P, CH]), PB[2 + c % 2][:, :],
                                       chunk(RA, c - 1)[:, CH - 1:CH] if c % CB else 0.0, ALU.mult, ALU.add)\
                   .then_inc(s["scanned"], 1)
                dve.wait_ge(s["scanned"], c + 1)
                dve.tensor_tensor(chunk(XS, c), chunk(RA, c), PB[c % 2][:, :], ALU.mult).then_inc(s["gated"], 1)

            def gate(c):
                dve.wait_ge(s["normed"], NC + c + 1)
                dve.tensor_scalar(chunk(XC, c), chunk(XC, c), vecA[:, 1:2], vecA[:, 2:3], ALU.mult, ALU.add)\
                   .then_inc(s["scaled"], 1)
                dve.wait_ge(s["scaled"], c + 1)
                dve.wait_ge(s["silu_ready"], c + 1)
                dve.tensor_tensor(chunk(XC, c), chunk(XC, c), chunk(RB, c), ALU.mult).then_inc(s["gatedmul"], 1)

            norm_vector(dve, 1, lambda c: chunk(XS, c), lambda c: chunk(XC, c), after=gate)
            for c in range(NC):
                dve.wait_ge(s["outA_ready"], c + 1)
                dve.tensor_tensor(chunk(X, c), chunk(X, c), PB[c % 2][:, :], ALU.add).then_inc(s["x1_ready"], 1)
            dve.wait_ge(s["x1_ready"], NC)
            norm_vector(dve, 2, lambda c: chunk(X, c), lambda c: inner(XL, c))
            dve.wait_ge(s["tables_in"], 32)
            dve.wait_ge(s["inner_copied"], NC)

            def step(u, i, have, last):
                b, j = divmod(i, CB)
                if have >= 1 and last != 2:
                    v = (i - 1) % UNITS
                    dve.wait_ge(s["scores"], done(u - 3))
                    if v % CB == 0:
                        dve.memset(kT[:, v % 2, 0:WIN], 0.0)
                    else:
                        dve.wait_ge(s["kready"], done(u - 2))
                        dve.tensor_scalar(kT[:, v % 2, 0:WIN], kT[:, 1 - v % 2, CH:CH + WIN], carry_f, None, ALU.mult)
                    dve.wait_ge(s["spreadk"], done(u - 1))
                    dve.wait_ge(s["ksumd"], done(u - 1))
                    dve.tensor_tensor(kT[:, v % 2, WIN:WIN + CH], ksum[:, :], PB[3][:, :], ALU.mult)\
                       .then_inc(s["kready"], 1)
                if have >= 2:
                    dve.wait_ge(s["ptrans"], done(u - 2))
                    dve.wait_ge(s["pv"], done(u - 3))
                    dve.tensor_copy(PT[:, :], PB[3][:, :]).then_inc(s["ptcopy"], 1)
                if not last:
                    tb = slice(j * CH, (j + 1) * CH)
                    dve.wait_ge(s["swapq"], done(u))
                    dve.wait_ge(s["sqd"], done(u - 1))
                    dve.wait_ge(s["qsum"], done(u - 1))
                    dve.scalar_tensor_tensor(tq[:, 1, :], tq[:, 1, :], qks[:, 1:2], TABQ[:, 1, tb], ALU.mult, ALU.mult)
                    dve.wait_ge(s["sqq"], done(u))
                    dve.scalar_tensor_tensor(tq[:, 0, :], PB[0][:, :], qks[:, 0:1], TABQ[:, 0, tb], ALU.mult, ALU.mult)\
                       .then_inc(s["rotq"], 1)
                if not last:
                    dve.wait_ge(s["swapk"], done(u))
                    dve.wait_ge(s["ksumd"], done(u - 1))
                    dve.scalar_tensor_tensor(tk[:, 1, :], tk[:, 1, :], qks[:, 3:4], TABK[:, 1, tb], ALU.mult, ALU.mult)
                    dve.wait_ge(s["sqd"], done(u))
                    dve.scalar_tensor_tensor(tk[:, 0, :], PB[1][:, :], qks[:, 2:3], TABK[:, 0, tb], ALU.mult, ALU.mult)\
                       .then_inc(s["rotk"], 1)
                if not last:
                    dve.wait_ge(s["ssq"], done(u))
                    dve.wait_ge(s["rnorm"], done(u - 1))
                    dve.tensor_scalar(ss[:, :].rearrange("p (b q h) -> p b q h", b=NBLK, q=2),
                                      PB[0][:, 0:256].rearrange("p (b q x) -> p b q x", b=NBLK, q=2)[:, :, :, 0:2],
                                      1e-24, None, ALU.max).then_inc(s["ssc"], 1)
                if have >= 1 and last != 2:
                    sc = QS[:, :].rearrange("p (h x) -> p h x", h=2)[:, :, 0:256].rearrange("p h (b n) -> p h b n", n=64)
                    dve.wait_ge(s["scores"], done(u - 1))
                    dve.wait_ge(s["shifted"], done(u - 2))
                    dve.tensor_reduce(mx[:, :].rearrange("p (h b) -> p h b", h=2), sc, AX.X, ALU.max)\
                       .then_inc(s["maxed"], 1)
                    dve.wait_ge(s["maxed"], done(u - 1))
                    for h in range(2):
                        m = dve.tensor_tensor(
                            S1[:, h * 256:(h + 1) * 256].rearrange("p (b n) -> p b n", b=NBLK),
                            sc[:, h], mx[:, h * NBLK:(h + 1) * NBLK].unsqueeze(2).to_broadcast([P, NBLK, 64]),
                            ALU.subtract)
                    m.then_inc(s["shifted"], 1)
                    dve.wait_ge(s["shifted"], done(u - 1))
                    dve.wait_ge(s["exped"], done(u - 2))
                    dve.wait_ge(s["rnorm"], done(u - 1))
                    for h in range(2):
                        m = dve.tensor_tensor(
                            S2[:, h * 256:(h + 1) * 256].rearrange("p (b n) -> p b n", b=NBLK),
                            S1[:, h * 256:(h + 1) * 256].rearrange("p (b n) -> p b n", b=NBLK),
                            rn[:, (i - 1) % 2, h:h + 13:4].unsqueeze(2).to_broadcast([P, NBLK, 64]), ALU.mult)
                    m.then_inc(s["scaledS"], 1)
                if have >= 2:
                    dve.wait_ge(s["yproj"], done(u - 2))
                    dve.tensor_tensor(inner(XN, (i - 2) % UNITS), inner(XN, (i - 2) % UNITS), PB[5][:, :], ALU.add)\
                       .then_inc(s["acc"], 1)
                if have >= 1 and last != 2:
                    dve.wait_ge(s["exped"], done(u - 1))
                    dve.wait_ge(s["recip"], done(u - 2))
                    dve.tensor_reduce(rs[:, :], EX[:, :].rearrange("p (g n) -> p g n", n=64), AX.X, ALU.add)\
                       .then_inc(s["summed"], 1)
                    dve.wait_ge(s["summed"], done(u - 1))
                    dve.wait_ge(s["pnorm"], done(u - 2))
                    dve.reciprocal(rr[:, :], rs[:, :]).then_inc(s["recip"], 1)

            with dve.Fori(0, DEPTH) as l:
                k = K_LAYER + l
                dve.wait_ge(s["qks_in"], (l + 1) * 16)
                run_units(dve, l, step, 2)
                dve.wait_ge(s["shiftF"], (l + 1) * NC)
                norm_vector(dve, k, lambda c: chunk(XS, c), lambda c: chunk(XS, c))
                for c in range(NC):
                    for f, (f0, fn) in enumerate(FT):
                        n = l * (3 * NC) + c * 3 + f
                        dve.wait_ge(s["gelu"], n + 1)
                        if c >= 2 and f == 0:
                            dve.wait_ge(s["down"], l * NC + c - 1)
                        dve.scalar_tensor_tensor(hh[0:fn, (c % 2) * 3 + f, :], PB[2 * ((c * 3 + f) % 2)][0:fn, :],
                                                 fvec[0:fn, 2 + f:3 + f], gl[0:fn, (c * 3 + f) % 2, :], ALU.add, ALU.mult)\
                           .then_inc(s["hmul"], 1)
                    if c >= 1:
                        layer_result(dve, l, c - 1)
                layer_result(dve, l, NC - 1)
                dve.wait_ge(s["layer_out"], (l + 1) * NC + 1)
                for c in range(NC):
                    m = dve.tensor_copy(inner(XN, c), inner(XL, c))
                m.then_inc(s["inner_copied"], 1)
                dve.wait_ge(s["inner_copied"], NC + l + 1)
            for c in range(NC):
                dve.tensor_tensor(chunk(X, c), chunk(X, c), inner(XL, c), ALU.add).then_inc(s["x2_ready"], 1)
            dve.wait_ge(s["x2_ready"], NC)
            norm_vector(dve, K_ATT, lambda c: chunk(X, c), lambda c: chunk(XC, c))
            for c in range(NC):
                if c >= 2:
                    dve.wait_ge(s[f"split_out{c % 2}"], 96 * (c // 2))
                for qk in range(2):
                    dve.wait_ge(s["c_hi"], 2 * c + qk + 1)
                    dve.tensor_tensor(REST[:, c % 2, qk, :], PB[(c % 2) * 3 + qk][:, :], SPL[:, c % 2, qk, 0, :],
                                      ALU.subtract).then_inc(s["c_rest"], 1)
                for qk in range(2):
                    dve.wait_ge(s["c_mid"], 2 * c + qk + 1)
                    dve.tensor_tensor(SPL[:, c % 2, qk, 2, :], REST[:, c % 2, qk, :], SPL[:, c % 2, qk, 1, :],
                                      ALU.subtract).then_inc(s["c_low"], 1)
            dve.wait_ge(s["c_vcopy"], NC)
            dve.memset(PB[4][:, :], 0.0).then_inc(s["o_zero"], 1)

            def first_max(g, n):
                h, qt, kc = FIRST[n]
                dve.wait_ge(s["score1"], g * len(FIRST) + n + 1)
                if n == 0 and not (isinstance(g, int) and g == 0):
                    dve.wait_ge(s["max_all"], g)
                dve.tensor_reduce(mxp[:, h, qt, kc:kc + 1], PB[2 + n % 2][:, 0:first_pass_keys(qt, kc)],
                                  AX.X, ALU.max).then_inc(s["max1"], 1)

            def split_max(g):
                dve.wait_ge(s["max1"], (g + 1) * len(FIRST))
                if not (isinstance(g, int) and g == 0):
                    dve.wait_ge(s["neg_turned"], g)
                for j in range(CB):
                    m = dve.tensor_reduce(mxa[:, :].rearrange("p (h q) -> p h q", h=GH)[:, :, 4 * j:4 * j + 4],
                                          mxp[:, :, 4 * j:4 * j + 4, 0:j + 1], AX.X, ALU.max)
                m.then_inc(s["max_all"], 1)
                dve.wait_ge(s["max_all"], g + 1)
                dve.tensor_scalar(nhi[:, :], mxa[:, :], -1.0, None, ALU.mult).then_inc(s["neg_hi"], 1)
                dve.wait_ge(s["neg_hi"], g + 1)
                dve.scalar_tensor_tensor(nrest[:, 0, :], mxa[:, :], -1.0, nhi[:, :], ALU.mult, ALU.subtract)\
                   .then_inc(s["neg_rest"], 1)
                dve.tensor_copy(nparts[:, 0, :], nhi[:, :])
                dve.wait_ge(s["neg_rest"], g + 1)
                dve.tensor_copy(nmid[:, :], nrest[:, 0, :]).then_inc(s["neg_mid"], 1)
                dve.wait_ge(s["neg_mid"], g + 1)
                dve.tensor_tensor(nparts[:, 2, :], nrest[:, 0, :], nmid[:, :], ALU.subtract)
                dve.tensor_copy(nparts[:, 1, :], nmid[:, :]).then_inc(s["neg_low"], 1)

            def copy_max(g, p2, loads):
                dve.wait_ge(s["neg_turned"], g + 1)
                if loads is not None:
                    dve.wait_ge(s[f"neg_rows{p2}"], 48 * loads)
                dve.tensor_copy(nT[:, 0, :], PB[5][:, 0:P])
                dve.tensor_copy(nT[0:64, 1, :], PB[5][0:64, P:2 * P]).then_inc(s["neg_copied"], 1)

            def copy_o(g, c):
                dve.wait_ge(s["pv2"], g * ITEMS + ITEM.index((c, 4 * c + 3)) + 3)
                dve.tensor_copy(oTs, PB[4][:, :]).then_inc(s["o_copied"], 1)

            def store_o(g, c, p, hg):
                dve.wait_ge(s["o_turned"], g * CB + c + 1)
                tv = PB[5][:, :].rearrange("p (b h x) -> p b h x", b=NBLK, h=GH)
                dve.reciprocal(o_inv[:, :].rearrange("p (b h x) -> p b h x", b=NBLK, h=GH), tv[:, :, :, 8:9])\
                   .then_inc(s["o_inv"], 1)
                dve.wait_ge(s["o_inv"], g * CB + c + 1)
                for b in range(NBLK):
                    m = dve.tensor_tensor(
                        OTOK[:, p * NT + 4 * c + b, bass.ds(hg * 32, 32)].rearrange("p (h d) -> p h d", h=GH),
                        tv[:, b, :, 0:8],
                        o_inv[:, b * GH:(b + 1) * GH].unsqueeze(2).to_broadcast([P, GH, 8]), ALU.mult)
                m.then_inc(s["o_stored"], 1)

            def att_step(g, p, hg, loads, g1=True, g2=True):
                for n in range(ITEMS):
                    if g1:
                        for x in range(NF // 2):
                            first_max(g, n * NF + x)
                    if g2 and n >= 1 and ends_chunk(n - 1):
                        copy_o(g - 1, ITEM[n - 1][0])
                    if g2 and n >= 2 and ends_chunk(n - 2):
                        store_o(g - 1, ITEM[n - 2][0], p, hg)
                    if g1:
                        for x in range(NF // 2, NF):
                            first_max(g, n * NF + x)
                if g2:
                    copy_o(g - 1, CB - 1)
                    store_o(g - 1, CB - 1, p, hg)
                if g1:
                    split_max(g)
                    copy_max(g, p, loads)

            dve.sem_inc(s["o_copied"], 1)
            dve.sem_inc(s["o_stored"], 1)
            att_step(0, None, None, None, True, False)
            with dve.Fori(1, NG // 2) as i:
                att_step(2 * i - 1, 0, i - 1, i)
                att_step(2 * i, 1, i - 1, i)
            att_step(NG - 1, 0, NG // 2 - 1, NG // 2)
            att_step(NG, 1, NG // 2 - 1, None, False, True)
            for c in range(NC):
                dve.wait_ge(s["out2"], c + 1)
                dve.tensor_tensor(chunk(X, c), chunk(X, c), PB[2 + c % 2][:, :], ALU.add).then_inc(s["x3_ready"], 1)
            dve.wait_ge(s["x3_ready"], NC)
            norm_vector(dve, K_MOE, lambda c: chunk(X, c), lambda c: chunk(XC, c))
            norm_vector(dve, K_RMS, lambda c: chunk(XC, c), lambda c: chunk(XS, c), center=False, eps=1e-8)
            for c in range(NC):
                dve.wait_ge(s["xtok_turned"], c + 1)
                dve.tensor_copy(XTOK[:, c * NBLK:(c + 1) * NBLK, :].rearrange("p b f -> p (b f)"), PB[4 + c % 2][:, :])\
                   .then_inc(s["xtok_copied"], 1)
            dve.wait_ge(s["probs"], 1)
            dve.wait_ge(s["rank_tri"], 3)
            pj = PR[:, :, :].unsqueeze(2).to_broadcast([P, NC * NBLK, NE, NE])
            pe_ = PR[:, :, :].unsqueeze(3).to_broadcast([P, NC * NBLK, NE, NE])
            dve.tensor_tensor(CMPA, pj, pe_, ALU.is_gt).then_inc(s["rank_gt"], 1)
            dve.tensor_tensor(CMPB, pj, pe_, ALU.is_equal).then_inc(s["rank_eq"], 1)
            dve.wait_ge(s["rank_eq"], 1)
            dve.tensor_tensor(CMPB, CMPB, tri_e[:, :, :].unsqueeze(1).to_broadcast([P, NC * NBLK, NE, NE]), ALU.mult)\
               .then_inc(s["rank_eq"], 1)
            dve.wait_ge(s["rank_gt"], 1)
            dve.tensor_reduce(RK[0][:, :, :], CMPA, AX.X, ALU.add).then_inc(s["rank_sum1"], 1)
            dve.wait_ge(s["rank_eq"], 2)
            dve.tensor_reduce(RK[1][:, :, :], CMPB, AX.X, ALU.add).then_inc(s["rank_sum2"], 1)
            dve.wait_ge(s["rank_sum2"], 1)
            dve.tensor_tensor(RK[0][:, :, :], RK[0][:, :, :], RK[1][:, :, :], ALU.add).then_inc(s["rank"], 1)
            dve.wait_ge(s["rank"], 1)
            dve.scalar_tensor_tensor(RK[1][:, :, :], RK[0][:, :, :], 2.0, PR[:, :, :], ALU.is_lt, ALU.mult)\
               .then_inc(s["chosen"], 1)
            dve.wait_ge(s["chosen"], 1)
            dve.tensor_reduce(wsum[:, :], RK[1][:, :, :], AX.X, ALU.add).then_inc(s["wsum"], 1)
            dve.wait_ge(s["wsum"], 1)
            dve.tensor_scalar(wsum[:, :], wsum[:, :], 1e-6, None, ALU.add).then_inc(s["wsum"], 1)
            dve.wait_ge(s["wsum"], 2)
            dve.reciprocal(wsum[:, :], wsum[:, :]).then_inc(s["winv"], 1)
            dve.wait_ge(s["winv"], 1)
            dve.tensor_tensor(CM[:, :, 0:NE], RK[1][:, :, :], wsum[:, :].unsqueeze(2).to_broadcast([P, NC * NBLK, NE]),
                              ALU.mult).then_inc(s["comb"], 1)
            dve.wait_ge(s["comb"], 1)
            dve.sem_inc(s["relu_v"], 2)
            dve.sem_inc(s["acc2"], 3)
            dve.sem_inc(s["comb_copied"], 1)
            dve.sem_inc(s["comb_cur"], 1)
            with dve.Fori(0, NC) as c:
                dve.wait_ge(s["comb_turned"], c + 1)
                dve.wait_ge(s["acc2"], c * (NE + 1) + 3)
                dve.tensor_copy(cmc[:, :, :], CM[:, bass.ds(c * NBLK, NBLK), :]).then_inc(s["comb_cur"], 1)
                dve.wait_ge(s["comb_turned"], c + 2)
                dve.wait_ge(s["down2"], c * (NE + 1) + 3)
                dve.tensor_copy(cmT, PB[7][0:9, :]).then_inc(s["comb_copied"], 1)
                for f in range(NE + 1):
                    it = c * (NE + 1) + f
                    dve.wait_ge(s["down2"], it + 1)
                    for j in (1, 3):
                        dve.wait_ge(s["up2"], it * HF + j + 1)
                        dve.tensor_scalar(HB[f % 3][:, j, :], PB[j][:, :], mvec[:, f * HF + j:f * HF + j + 1], 0.0,
                                          ALU.add, ALU.max).then_inc(s["relu_v"], 1)
                    if f:
                        add_expert(c, f - 1)
                add_expert(c, NE)


        @block.tensor
        def _(pe):
            def out_c(c):
                pe.wait_ge(s["oF_copied"], c + 1)
                if c >= 2:
                    pe.wait_ge(s["x3_ready"], c - 1)
                pe.matmul(PB[2 + c % 2][:, :], wC[:, 3, :], chunk(XS, c), start=True, stop=True).then_inc(s["out2"], 1)

            def second_layer(c, f):
                it = c * (NE + 1) + f
                pe.wait_ge(s["relu_a"], 2 * it + 4)
                pe.wait_ge(s["relu_v"], 2 * it + 4)
                pe.wait_ge(s["acc2"], it + 1)
                w = SW2 if f == 0 else EW2[:, f - 1]
                if f == 0:
                    pe.wait_ge(s["comb_copied"], c + 2)
                for b in range(NBLK):
                    for k in range(HF):
                        m = pe.matmul(PB[4 + f % 3][:, b * P:(b + 1) * P], HB[f % 3][:, k, b * P:(b + 1) * P], w[:, k, :],
                                      start=(k == 0), stop=(k == HF - 1 and f > 0))
                    if f == 0:
                        m = pe.matmul(PB[4][:, b * P:(b + 1) * P], cmT[:, b * P:(b + 1) * P], bias2[:, :],
                                      start=False, stop=True)
                m.then_inc(s["down2"], 1)

            for name in ("projq", "projk", "ssrow", "ssq", "spreadk", "scores", "ptrans", "vproj0", "vproj1", "pv", "yproj"):
                pe.sem_inc(s[name], CREDIT)
            pe.wait_ge(s["const_in"], 16)
            pe.wait_ge(s["x_in"], 16)
            for c in range(NC):
                if c >= 2:
                    pe.wait_ge(s["x_turned"], c - 1)
                for j in range(NBLK):
                    m = pe.transpose(PB[c % 2][:, j * P:(j + 1) * P], TOK[:, c * NBLK + j, :], ident)
                m.then_inc(s["x_blocks"], 1)
            pe.wait_ge(s["x_turned"], NC)
            norm_tensor(pe, 0, lambda c: chunk(X, c), "x_turned", lambda c: c + 1)
            pe.wait_ge(s["wA_in"], 32)
            for c in range(NC):
                pe.wait_ge(s["normed"], c + 1)
                if c >= 2:
                    pe.wait_ge(s["gated"], c - 1)
                    pe.wait_ge(s["silu_ready"], c - 1)
                else:
                    pe.wait_ge(s["normed"], NC - 1 + c)
                pe.matmul(PB[c % 2][:, :], wA[:, 0, :], chunk(XC, c), start=True, stop=True)
                pe.matmul(PB[2 + c % 2][:, :], wA[:, 1, :], chunk(XC, c), start=True, stop=True)
                pe.matmul(PB[4 + c % 2][:, :], wA[:, 2, :], chunk(XC, c), start=True, stop=True)\
                  .then_inc(s["projA_ready"], 1)
            pe.wait_ge(s["gated"], NC)
            norm_tensor(pe, 1, lambda c: chunk(XS, c), "gated", lambda c: c + 1)
            for c in range(NC):
                pe.wait_ge(s["gatedmul"], max(c + 1, min(NC, c + NC - 1) if c < 2 else c + 1))
                if c >= 2:
                    pe.wait_ge(s["x1_ready"], c - 1)
                pe.matmul(PB[c % 2][:, :], wA[:, 3, :], chunk(XC, c), start=True, stop=True).then_inc(s["outA_ready"], 1)
            pe.wait_ge(s["x1_ready"], NC)
            norm_tensor(pe, 2, lambda c: chunk(X, c), "x1_ready", lambda c: c + 1)

            def step(u, i, have, last):
                if not last:
                    if i == 0:
                        pe.wait_ge(s["pair_in"], pair_count(u) * 16)
                    pe.wait_ge(s["xs_ready"], done(u) + layer_no[0])
                    pe.wait_ge(s["rotq"], done(u - 1))
                    pe.wait_ge(s["ssc"], done(u - 1))
                    xm = xs[:, i % 2, WIN:WIN + CH]
                    pe.matmul(PB[0][:, :], wqkv[:, 0:P], xm, start=True, stop=True).then_inc(s["projq"], 1)
                if have >= 1 and last != 2:
                    pe.wait_ge(s["rnwide"], done(u - 1))
                    pe.wait_ge(s["ptcopy"], done(u - 3))
                    for blk in range(NBLK):
                        m = pe.transpose(PB[3][:, blk * P:(blk + 1) * P], rnx[:, blk, :], ident)
                    m.then_inc(s["spreadk"], 1)
                if not last:
                    pe.wait_ge(s["vcopy0"], done(u - 1))
                    v_windows(i, range(0, 8)).then_inc(s["vproj0"], 1)
                if have >= 2:
                    pe.wait_ge(s["pnorm"], done(u - 2))
                    pe.wait_ge(s["kready"], done(u - 1 if last != 2 else u - 2))
                    pe.wait_ge(s["acc"], done(u - 3))
                    for blk in range(NBLK):
                        m = pe.transpose(PB[3][:, blk * P:(blk + 1) * P], PN[:, blk * P:(blk + 1) * P], ident)
                    m.then_inc(s["ptrans"], 1)
                if not last:
                    pe.wait_ge(s["rotk"], done(u - 1))
                    pe.matmul(PB[1][:, :], wqkv[:, P:2 * P], xm, start=True, stop=True).then_inc(s["projk"], 1)
                if have >= 2:
                    pe.wait_ge(s["const_ready"], 2)
                    pe.wait_ge(s["ptcopy"], done(u - 2))
                    pe.wait_ge(s["vcopy1"], done(u - 2))
                    values(i, 0)
                if not last:
                    pe.wait_ge(s["sqd"], done(u))
                    pe.wait_ge(s["rotq"], done(u))
                    pe.matmul(PB[0][0:32, :], headsel, sqh[:, 0, :], start=True, stop=True)
                    pe.matmul(PB[0][32:64, :], headsel, sqh[:, 1, :], start=True, stop=True).then_inc(s["ssrow"], 1)
                if have >= 2:
                    values(i, 1).then_inc(s["pv"], 1)
                if not last:
                    pe.wait_ge(s["const_ready"], 2)
                    pe.wait_ge(s["sscopy"], done(u))
                    for blk in range(NBLK):
                        m = pe.transpose(PB[0][:, blk * 64:(blk + 1) * 64], ssT[:, blk * P:(blk + 1) * P],
                                         con[0:64, 0:64])
                    m.then_inc(s["ssq"], 1)
                    pe.wait_ge(s["vcopy1"], done(u - 1))
                    v_windows(i, range(8, 12))
                if have >= 1 and last != 2:
                    v = (i - 1) % UNITS
                    pe.wait_ge(s["kready"], done(u - 1))
                    pe.wait_ge(s["qsum"], done(u - 1))
                    pe.wait_ge(s["shifted"], done(u - 2))
                    mk = mask_b[:, 0 if v % CB == 0 else 1, :]
                    for h in range(2):
                        pe.matmul(QS[:, h * CH:h * CH + 256], ident_b[:, :], mk, start=True, stop=False,
                                  skip_group_check=True)
                    for h in range(2):
                        hs = slice(64 * h, 64 * h + 64)
                        for w in range(NWIN):
                            blk, r = divmod(w, NBLK)
                            m = pe.matmul(QS[32 * r:32 * r + 32, h * CH + blk * 64:h * CH + blk * 64 + 64],
                                          qT[hs, v % 2, w * WIN:(w + 1) * WIN], kT[hs, v % 2, w * WIN:w * WIN + 2 * WIN],
                                          start=False, stop=(blk == NBLK - 1), skip_group_check=True)
                    m.then_inc(s["scores"], 1)
                if have >= 2:
                    if i == 2:
                        pe.wait_ge(s["wo_in"], pair_count(u - 2) * 16)
                    pe.wait_ge(s["ocopy"], done(u - 2))
                    pe.matmul(PB[5][:, :], wo[:, :], oT[:, :], start=True, stop=True).then_inc(s["yproj"], 1)
                if not last:
                    v_windows(i, range(12, 16)).then_inc(s["vproj1"], 1)

            def values(i, half):
                for h in range(2):
                    for w in range(8 * half, 8 * half + 8):
                        hs = slice(64 * h, 64 * h + 64)
                        m = pe.matmul(PB[5][hs, w * WIN:(w + 1) * WIN], V2[hs, i % 2, w * DH:(w + 1) * DH],
                                      PT[hs, w * WIN:(w + 1) * WIN], start=True, stop=True)
                return m

            def v_windows(i, windows):
                for win in windows:
                    bank, w = (PB[4], win) if win < 8 else (PB[2], win - 8)
                    for h in range(2):
                        m = pe.matmul(bank[64 * h:64 * h + 64, w * DH:(w + 1) * DH], xs[:, i % 2, win * WIN:win * WIN + 64],
                                      wqkv[:, 2 * P + 64 * h:2 * P + 64 * h + 64], start=True, stop=True)
                return m

            pair_no, layer_no = [None], [None]

            def pair_count(u):
                return pair_no[0]

            def steps(l):
                base = l * (PAIRS * UNITS)
                layer_no[0] = l
                pair_no[0] = l * PAIRS + 1
                for i in range(UNITS):
                    step(base + i, i, min(i, 2), 0)
                with pe.Fori(1, PAIRS) as pr:
                    pair_no[0] = l * PAIRS + pr + 1
                    for i in range(UNITS):
                        step(base + pr * UNITS + i, i, 2, 0)
                for i in range(2):
                    step(base + PAIRS * UNITS + i, i, 2, 1 + i)

            pe.wait_ge(s["const_ready"], 2)
            with pe.Fori(0, DEPTH) as l:
                steps(l)
                k = K_LAYER + l
                norm_tensor(pe, k, lambda c: chunk(XS, c), "shiftF", lambda c: l * NC + c + 1)
                pe.wait_ge(s["ffw_in"], (l + 1) * 48)
                for c in range(NC):
                    pe.wait_ge(s["affine"], l * NC + c + 1)
                    for f, (f0, fn) in enumerate(FT):
                        n = c * 3 + f
                        if n >= 2:
                            pe.wait_ge(s["hmul"], l * (3 * NC) + n + 1)
                        else:
                            pe.wait_ge(s["normed"], (k + 1) * NC)
                        pe.matmul(PB[2 * (n % 2)][0:fn, :], w1[:, f0:f0 + fn], chunk(XC, c), start=True, stop=True)
                        pe.matmul(PB[2 * (n % 2) + 1][0:fn, :], w1[:, FF + f0:FF + f0 + fn], chunk(XC, c),
                                  start=True, stop=True).then_inc(s["up"], 1)
                    if c >= 1:
                        down(pe, l, c - 1)
                down(pe, l, NC - 1)
                pe.wait_ge(s["layer_out"], (l + 1) * NC + 1)
            pe.wait_ge(s["w1att_in"], 16)
            norm_tensor(pe, K_ATT, lambda c: chunk(X, c), "x2_ready", lambda c: c + 1)
            for c in range(NC):
                pe.wait_ge(s["normed"], K_ATT * NC + (c + 1 if c >= 2 else NC))
                if c >= 2:
                    pe.wait_ge(s["c_rest"], 2 * (c - 1))
                    pe.wait_ge(s["c_vcopy"], c - 1)
                bk = (c % 2) * 3
                pe.matmul(PB[bk][:, :], wC[:, 0, :], chunk(XC, c), start=True, stop=True)
                pe.matmul(PB[bk + 1][:, :], wC[:, 1, :], chunk(XC, c), start=True, stop=True)
                for b in range(NBLK):
                    m = pe.matmul(PB[bk + 2][:, b * P:(b + 1) * P], XC[:, c * CH + b * P:c * CH + (b + 1) * P], wC[:, 2, :],
                                  start=True, stop=True)
                m.then_inc(s["c_proj"], 1)
            pe.wait_ge(s["tri_ready"], 4)
            pe.wait_ge(s["o_zero"], 1)
            pe.wait_ge(s["c_rest"], 2 * NC)

            def first_pass(g, p, n):
                h, qt, kc = FIRST[n]
                keys = first_pass_keys(qt, kc)
                if not (isinstance(g, int) and g == 0 and n < 2):
                    pe.wait_ge(s["max1"], g * len(FIRST) + n - 1)
                diag = kc == qt // 4
                bank = PB[2 + n % 2]
                m = pe.matmul(bank[:, 0:keys], QST[p][0:KR, h * SEQ + qt * P:h * SEQ + (qt + 1) * P],
                              KST[p][0:KR, h * SEQ + kc * CH:h * SEQ + kc * CH + keys], start=True, stop=not diag)
                if diag:
                    m = pe.matmul(bank[:, keys - P:keys], ident_b[:, :], tri_q[:, :], start=False, stop=True)
                m.then_inc(s["score1"], 1)

            def second_scores(g, p, n):
                c, kt = ITEM[n]
                r = max(0, kt - 4 * c)
                for half in range(2):
                    it = g * ITEMS + n
                    pe.wait_ge(s["exp2"], 2 * it + half + 1)
                    for x in range(2):
                        h = 2 * half + x
                        q0 = h * SEQ + c * CH + r * P
                        m = pe.matmul(ST2[half][:, x, 0:CH - r * P], KST[p][0:KR + 3, h * SEQ + kt * P:h * SEQ + (kt + 1) * P],
                                      QST[p][0:KR + 3, q0:q0 + CH - r * P], start=True, stop=kt < 4 * c)
                        if kt >= 4 * c:
                            m = pe.matmul(ST2[half][:, x, 0:P], ident_b[:, :], tri_k[:, :], start=False, stop=True)
                    m.then_inc(s["score2"], 1)

            def second_values(g, p, n):
                c, kt = ITEM[n]
                r = max(0, kt - 4 * c)
                pe.wait_ge(s["exp2"], 2 * (g * ITEMS + n + 1) + 2)
                if kt == 0:
                    pe.wait_ge(s["o_copied"], g * CB + c + 1)
                for h in range(GH):
                    m = pe.matmul(PB[4][32 * h:32 * h + 9, r * P:CH], VG[p][:, h, kt, :], PTE[n % 2][:, h, 0:CH - r * P],
                                  start=(kt == 0), stop=(kt == 4 * c + 3), skip_group_check=True)
                m.then_inc(s["pv2"], 1)

            def turn_o(g, c):
                pe.wait_ge(s["o_copied"], g * CB + c + 2)
                pe.wait_ge(s["neg_copied"], g + 1)
                pe.wait_ge(s["o_stored"], g * CB + c + 1)
                for b in range(NBLK):
                    m = pe.transpose(PB[5][:, b * P:(b + 1) * P], oTs[:, b * P:(b + 1) * P], ident)
                m.then_inc(s["o_turned"], 1)

            def att_step(g, p1, loads1, loads2, g1=True, g2=True):
                p2 = 1 - p1
                if g1:
                    pe.wait_ge(s[f"stacks_in{p1}"], 192 * loads1)
                if g2:
                    pe.wait_ge(s[f"neg_rows{p2}"], 48 * loads2)
                    pe.wait_ge(s["vgroup"], g)
                for n in range(ITEMS):
                    if g2:
                        second_scores(g - 1, p2, n)
                    if g1:
                        for x in range(NF // 2):
                            first_pass(g, p1, n * NF + x)
                    if g2:
                        if n:
                            second_values(g - 1, p2, n - 1)
                            if n >= 2 and ends_chunk(n - 2):
                                turn_o(g - 1, ITEM[n - 2][0])
                    if g1:
                        for x in range(NF // 2, NF):
                            first_pass(g, p1, n * NF + x)
                if g2:
                    second_values(g - 1, p2, ITEMS - 1)
                    turn_o(g - 1, CB - 1)
                if g1:
                    pe.wait_ge(s["neg_low"], g + 1)
                    if g2:
                        pe.wait_ge(s["o_stored"], g * CB + 1)
                    pe.transpose(PB[5][:, 0:P], nparts[:, 0:2, :].rearrange("p a n -> p (a n)"), ident)
                    pe.transpose(PB[5][0:64, P:2 * P], nparts[:, 2, :], ident).then_inc(s["neg_turned"], 1)

            pe.sem_inc(s["pv2"], 2)
            att_step(0, 0, 1, None, True, False)
            with pe.Fori(1, NG // 2) as i:
                att_step(2 * i - 1, 1, i, i)
                att_step(2 * i, 0, i + 1, i)
            att_step(NG - 1, 1, NG // 2, NG // 2)
            att_step(NG, 0, None, NG // 2, False, True)
            pe.wait_ge(s["o_stored"], NG * CB + 1)
            for c in range(NC):
                if c >= 2:
                    pe.wait_ge(s["oF_copied"], c - 1)
                for b in range(NBLK):
                    m = pe.transpose(PB[c % 2][:, b * P:(b + 1) * P], OTOK[:, c * NBLK + b, :], ident)
                m.then_inc(s["oF_turned"], 1)
                if c:
                    out_c(c - 1)
            out_c(NC - 1)
            pe.wait_ge(s["x3_ready"], NC)
            norm_tensor(pe, K_MOE, lambda c: chunk(X, c), "x3_ready", lambda c: c + 1)
            norm_tensor(pe, K_RMS, lambda c: chunk(XC, c), "normed", lambda c: K_MOE * NC + c + 1, center=False)
            for c in range(NC):
                if c >= 2:
                    pe.wait_ge(s["xtok_copied"], c - 1)
                for b in range(NBLK):
                    m = pe.transpose(PB[4 + c % 2][:, b * P:(b + 1) * P], X[:, c * CH + b * P:c * CH + (b + 1) * P], ident)
                m.then_inc(s["xtok_turned"], 1)
            pe.wait_ge(s["moew_in"], 16 * 7)
            for c in range(NC):
                pe.wait_ge(s["rms_scaled"], c + 1)
                for b in range(NBLK):
                    n = c * NBLK + b
                    m = pe.matmul(PB[6][:, n * NE:(n + 1) * NE], XS[:, n * P:(n + 1) * P], routw[:, :], start=True, stop=True)
            m.then_inc(s["logits"], 1)
            pe.wait_ge(s["comb"], 1)
            pe.wait_ge(s["xtok_copied"], NC)
            pe.sem_inc(s["comb_turned"], 1)
            pe.sem_inc(s["down2"], 3)
            with pe.Fori(0, NC) as c:
                pe.wait_ge(s["comb_cur"], c + 2)
                pe.wait_ge(s["comb_copied"], c + 1)
                for b in range(NBLK):
                    m = pe.transpose(PB[7][0:9, b * P:(b + 1) * P], cmc[:, b, :], ident)
                m.then_inc(s["comb_turned"], 1)
                for f in range(NE + 1):
                    it = c * (NE + 1) + f
                    for j in range(HF):
                        pe.wait_ge(s["relu_a" if j % 2 == 0 else "relu_v"], 2 * it + j // 2 + 1)
                        w = SW1 if f == 0 else EW1[:, f - 1, :]
                        pe.matmul(PB[j][:, :], w[:, j * P:(j + 1) * P], XS[:, bass.ds(c * CH, CH)], start=True, stop=True)\
                          .then_inc(s["up2"], 1)
                    if f:
                        second_layer(c, f - 1)
                second_layer(c, NE)

    

def rotary_tables(np):
    f = np.float32
    dim, seq, ch, win = 64, 2048, 512, 32
    half = np.arange(0, dim, 2, dtype=f)
    inv = f(1.0) / np.power(f(10000.0), half / f(dim)).astype(f)
    tt = np.arange(seq, dtype=f)
    fr = (tt[:, None] * inv[None, :]).astype(f)
    base = ((half + f(0.4 * dim)) / f(1.4 * dim)).astype(f).astype(np.float64)
    power = ((np.arange(seq) % ch) - ch // 2) / (win // 2)
    sc = base[None, :] ** power[:, None]
    cos, sin = np.cos(fr.astype(np.float64)), np.sin(fr.astype(np.float64))

    def full(a, b):
        one = np.concatenate([a, b], 1).T
        return np.concatenate([one, one], 0)
    tabs = np.stack([full(cos * sc, cos * sc), full(-sin * sc, sin * sc),
                     full(cos / sc, cos / sc), full(-sin / sc, sin / sc)]).astype(f)
    carry = np.tile(np.concatenate([base, base]) ** (ch / (win // 2)), 2).astype(f)
    return tabs, carry


def constants(np, carry):
    con = np.zeros((128, 417), np.float32)
    con[:, 0:128] = np.eye(128)
    con[:, 128:256] = 1.0 / 128
    con[0:64, 256] = 1
    con[64:128, 257] = 1
    con[:, 288] = carry
    r = np.arange(128)[:, None] % 32
    kk = np.arange(64)[None, :] - 32
    ok = (kk <= r) & (kk >= r - 32)
    con[:, 353:417] = np.where(ok, 0.0, -1e25)
    first = ok & ~((np.arange(128)[:, None] < 32) & (kk < 0))
    con[:, 289:353] = np.where(first, 0.0, -1e25)
    return con


def lay_out(np, i):
    a = {k: np.asarray(v) for k, v in i.items()}
    tabs, carry = rotary_tables(np)
    d = {"con": constants(np, carry), "tabs": tabs}
    d["x"] = a["L0_attn_x"].reshape(4096, 128)
    d["wA"] = np.stack([a["L0_attn_W" + n].T for n in "qvgo"], 1)
    d["vecA"] = np.stack([np.repeat(a["L0_attn_decay"][:, 1, 0], 8), a["L0_attn_ln_g"], a["L0_attn_ln_b"]], 1)
    W = a["L0_ffn_Wqkv"].reshape(6, 128, 3, 8, 2, 2, 32)
    parts = [W[:, :, 0], W[:, :, 1], W[:, :, 2]]
    d["Wqkv"] = np.stack([p.reshape(6, 128, 8, 128) for p in parts], 3).transpose(0, 2, 1, 3, 4).reshape(48, 128, 384)
    d["Wo"] = a["L0_ffn_Wo"].reshape(48, 128, 128)

    def two(v):
        return np.concatenate([v, v], 1)
    qs, ks = a["L0_ffn_q_scale"], a["L0_ffn_k_scale"]
    sw = lambda v: v.reshape(6, 2, 32)[:, ::-1].reshape(6, 64)
    d["qks"] = np.stack([two(qs), two(sw(qs)), two(ks), two(sw(ks))], 2)
    d["W1"] = a["L0_ffn_W1"]
    W2 = np.zeros((6, 384, 128), np.float32)
    W2[:, :341] = a["L0_ffn_W2"]
    d["W2"] = W2.reshape(6, 3, 128, 128).transpose(0, 2, 1, 3)
    b1 = np.zeros((6, 2, 384), np.float32)
    b1[:, :, :341] = a["L0_ffn_b1"].reshape(6, 2, 341)
    b1 = b1.reshape(6, 6, 128).transpose(0, 2, 1)
    d["fvec"] = np.concatenate([a["L0_ffn_ln_g"][:, :, None], a["L0_ffn_ln_b"][:, :, None], b1,
                                a["L0_ffn_b2"][:, :, None]], 2)
    d["wC"] = np.stack([a["L1_attn_W" + n].T for n in "qkvo"], 1)
    d["ew1"] = a["L1_ffn_ew1"]
    d["ew2"] = a["L1_ffn_ew2"].reshape(8, 4, 128, 128).transpose(2, 0, 1, 3)
    d["sw1"] = a["L1_ffn_sw1"]
    d["sw2"] = a["L1_ffn_sw2"].reshape(4, 128, 128).transpose(1, 0, 2)
    b1 = np.concatenate([a["L1_ffn_sb1"][None], a["L1_ffn_eb1"]], 0).reshape(36, 128)
    d["mvec"] = np.concatenate([b1, a["L1_ffn_norm_weight"][None]], 0).T
    d["bias2"] = np.concatenate([a["L1_ffn_eb2"], a["L1_ffn_sb2"][None]], 0)
    d["routw"] = a["L1_ffn_router_w"].T
    return {k: np.ascontiguousarray(v) for k, v in d.items()}


def kernel(**inputs):
    import numpy as _np
    import concourse.bacc as _bacc
    from concourse import mybir as _mybir
    from concourse.bass_utils import run_bass_kernel_spmd as _run

    nc = _bacc.Bacc("TRN2", target_bir_lowering=False, num_devices=1)
    arrays = lay_out(_np, inputs)
    t = {n: nc.dram_tensor(n + "_dram", v.shape, _mybir.dt.from_np(v.dtype), kind="ExternalInput").ap()
         for n, v in arrays.items()}
    out = nc.dram_tensor("out_dram", (4096, 128), _mybir.dt.float32, kind="ExternalOutput").ap()
    scr = nc.dram_tensor("parts_dram", (2, 2, 16, 3, 8, 2048), _mybir.dt.bfloat16, kind="Internal").ap()
    build_program(nc, t, out, scr)
    r = _run(nc, [{n + "_dram": v for n, v in arrays.items()}], core_ids=[0])
    return r.results[0]["out_dram"].reshape(2, 2048, 128)
```
